# Optimizing a Trainium2 kernel written in Bass

```python
import numpy as np
import jax
import jax.numpy as jnp

def _softmax(x, axis=-1):
    return jax.nn.softmax(x, axis=axis)

def _gelu(x):
    return jax.nn.gelu(x, approximate=True)

def _silu(x):
    return jax.nn.silu(x)

def _sigmoid(x):
    return jax.nn.sigmoid(x)

def _layernorm(x, axis=-1, eps=1e-05):
    m = jnp.mean(x, axis=axis, keepdims=True)
    v = jnp.var(x, axis=axis, keepdims=True)
    return (x - m) / jnp.sqrt(v + eps)

def _scatter_add(tgt, idx, src, axis=0):
    return tgt.at[idx].add(src)

def _segment_sum(src, seg, n):
    return jax.ops.segment_sum(src, seg, n)
kernel_name = 'mk_dlrm_tower_d1_rec_r8_7b6139'

def setup_inputs(seed: int=0):
    np.random.seed(seed)
    _w = jnp.asarray

    def _rec_inputs():
        import jax
        import jax.numpy as jnp
        _tk = jax.random.key(seed)
        dense_ctx = jax.random.normal(jax.random.fold_in(_tk, 190), (512, 16), jnp.float32)
        ids = jnp.stack([jax.random.randint(jax.random.fold_in(_tk, 200 + f), (512,), 0, v, jnp.int32) for f, v in enumerate([12500, 1250, 1250, 1250, 1250, 1250, 125000, 1000, 1250, 12500, 1250, 125000, 1000, 125000, 1000, 12500, 12500, 125000, 1000, 125000, 1250, 1250, 1000, 1000, 125000, 12500, 125000, 12500, 1250, 125000, 1250, 12500, 125000, 1250, 125000, 125000, 1250, 1000, 125000])], axis=1)
        tbl_0 = 0.05 * jax.random.normal(jax.random.fold_in(_tk, 500 + 0), (12500, 16), jnp.float32)
        tbl_1 = 0.05 * jax.random.normal(jax.random.fold_in(_tk, 500 + 1), (1250, 16), jnp.float32)
        tbl_2 = 0.05 * jax.random.normal(jax.random.fold_in(_tk, 500 + 2), (1250, 16), jnp.float32)
        tbl_3 = 0.05 * jax.random.normal(jax.random.fold_in(_tk, 500 + 3), (1250, 16), jnp.float32)
        tbl_4 = 0.05 * jax.random.normal(jax.random.fold_in(_tk, 500 + 4), (1250, 16), jnp.float32)
        tbl_5 = 0.05 * jax.random.normal(jax.random.fold_in(_tk, 500 + 5), (1250, 16), jnp.float32)
        tbl_6 = 0.05 * jax.random.normal(jax.random.fold_in(_tk, 500 + 6), (125000, 16), jnp.float32)
        tbl_7 = 0.05 * jax.random.normal(jax.random.fold_in(_tk, 500 + 7), (1000, 16), jnp.float32)
        tbl_8 = 0.05 * jax.random.normal(jax.random.fold_in(_tk, 500 + 8), (1250, 16), jnp.float32)
        tbl_9 = 0.05 * jax.random.normal(jax.random.fold_in(_tk, 500 + 9), (12500, 16), jnp.float32)
        tbl_10 = 0.05 * jax.random.normal(jax.random.fold_in(_tk, 500 + 10), (1250, 16), jnp.float32)
        tbl_11 = 0.05 * jax.random.normal(jax.random.fold_in(_tk, 500 + 11), (125000, 16), jnp.float32)
        tbl_12 = 0.05 * jax.random.normal(jax.random.fold_in(_tk, 500 + 12), (1000, 16), jnp.float32)
        tbl_13 = 0.05 * jax.random.normal(jax.random.fold_in(_tk, 500 + 13), (125000, 16), jnp.float32)
        tbl_14 = 0.05 * jax.random.normal(jax.random.fold_in(_tk, 500 + 14), (1000, 16), jnp.float32)
        tbl_15 = 0.05 * jax.random.normal(jax.random.fold_in(_tk, 500 + 15), (12500, 16), jnp.float32)
        tbl_16 = 0.05 * jax.random.normal(jax.random.fold_in(_tk, 500 + 16), (12500, 16), jnp.float32)
        tbl_17 = 0.05 * jax.random.normal(jax.random.fold_in(_tk, 500 + 17), (125000, 16), jnp.float32)
        tbl_18 = 0.05 * jax.random.normal(jax.random.fold_in(_tk, 500 + 18), (1000, 16), jnp.float32)
        tbl_19 = 0.05 * jax.random.normal(jax.random.fold_in(_tk, 500 + 19), (125000, 16), jnp.float32)
        tbl_20 = 0.05 * jax.random.normal(jax.random.fold_in(_tk, 500 + 20), (1250, 16), jnp.float32)
        tbl_21 = 0.05 * jax.random.normal(jax.random.fold_in(_tk, 500 + 21), (1250, 16), jnp.float32)
        tbl_22 = 0.05 * jax.random.normal(jax.random.fold_in(_tk, 500 + 22), (1000, 16), jnp.float32)
        tbl_23 = 0.05 * jax.random.normal(jax.random.fold_in(_tk, 500 + 23), (1000, 16), jnp.float32)
        tbl_24 = 0.05 * jax.random.normal(jax.random.fold_in(_tk, 500 + 24), (125000, 16), jnp.float32)
        tbl_25 = 0.05 * jax.random.normal(jax.random.fold_in(_tk, 500 + 25), (12500, 16), jnp.float32)
        tbl_26 = 0.05 * jax.random.normal(jax.random.fold_in(_tk, 500 + 26), (125000, 16), jnp.float32)
        tbl_27 = 0.05 * jax.random.normal(jax.random.fold_in(_tk, 500 + 27), (12500, 16), jnp.float32)
        tbl_28 = 0.05 * jax.random.normal(jax.random.fold_in(_tk, 500 + 28), (1250, 16), jnp.float32)
        tbl_29 = 0.05 * jax.random.normal(jax.random.fold_in(_tk, 500 + 29), (125000, 16), jnp.float32)
        tbl_30 = 0.05 * jax.random.normal(jax.random.fold_in(_tk, 500 + 30), (1250, 16), jnp.float32)
        tbl_31 = 0.05 * jax.random.normal(jax.random.fold_in(_tk, 500 + 31), (12500, 16), jnp.float32)
        tbl_32 = 0.05 * jax.random.normal(jax.random.fold_in(_tk, 500 + 32), (125000, 16), jnp.float32)
        tbl_33 = 0.05 * jax.random.normal(jax.random.fold_in(_tk, 500 + 33), (1250, 16), jnp.float32)
        tbl_34 = 0.05 * jax.random.normal(jax.random.fold_in(_tk, 500 + 34), (125000, 16), jnp.float32)
        tbl_35 = 0.05 * jax.random.normal(jax.random.fold_in(_tk, 500 + 35), (125000, 16), jnp.float32)
        tbl_36 = 0.05 * jax.random.normal(jax.random.fold_in(_tk, 500 + 36), (1250, 16), jnp.float32)
        tbl_37 = 0.05 * jax.random.normal(jax.random.fold_in(_tk, 500 + 37), (1000, 16), jnp.float32)
        tbl_38 = 0.05 * jax.random.normal(jax.random.fold_in(_tk, 500 + 38), (125000, 16), jnp.float32)
        _rk = jax.random.fold_in(_tk, 7)
        W_top1 = 0.05 * jax.random.normal(jax.random.fold_in(_tk, 801), (400, 512), jnp.float32)
        W_top2 = 0.0441942 * jax.random.normal(jax.random.fold_in(_tk, 802), (512, 256), jnp.float32)
        W_top3 = 0.0625 * jax.random.normal(jax.random.fold_in(_tk, 803), (256, 1), jnp.float32)
        b_top1 = jnp.zeros((512,), jnp.float32)
        b_top2 = jnp.zeros((256,), jnp.float32)
        return (dense_ctx, ids, tbl_0, tbl_1, tbl_2, tbl_3, tbl_4, tbl_5, tbl_6, tbl_7, tbl_8, tbl_9, tbl_10, tbl_11, tbl_12, tbl_13, tbl_14, tbl_15, tbl_16, tbl_17, tbl_18, tbl_19, tbl_20, tbl_21, tbl_22, tbl_23, tbl_24, tbl_25, tbl_26, tbl_27, tbl_28, tbl_29, tbl_30, tbl_31, tbl_32, tbl_33, tbl_34, tbl_35, tbl_36, tbl_37, tbl_38, W_top1, b_top1, W_top2, b_top2, W_top3)
    dense_ctx, ids, tbl_0, tbl_1, tbl_2, tbl_3, tbl_4, tbl_5, tbl_6, tbl_7, tbl_8, tbl_9, tbl_10, tbl_11, tbl_12, tbl_13, tbl_14, tbl_15, tbl_16, tbl_17, tbl_18, tbl_19, tbl_20, tbl_21, tbl_22, tbl_23, tbl_24, tbl_25, tbl_26, tbl_27, tbl_28, tbl_29, tbl_30, tbl_31, tbl_32, tbl_33, tbl_34, tbl_35, tbl_36, tbl_37, tbl_38, W_top1, b_top1, W_top2, b_top2, W_top3 = _rec_inputs()

    def _L0_rec_setup():
        import jax, jax.numpy as jnp
        import numpy as np
        B, F0, D = (512, 39, 16)
        CIN = [128, 128, 128]

        def _cin_layer(X0, Xi, W, b):
            H = W.shape[0]
            F0_, Fi = (X0.shape[1], Xi.shape[1])
            Wr = W.reshape(H, F0_, Fi)
            return jnp.einsum('hjk,bjd,bkd->bhd', Wr, X0, Xi) + b[None, :, None]
        key = jax.random.key(seed)
        ks = jax.random.split(key, 4)
        x = jax.random.normal(ks[0], (B, F0, D), dtype=jnp.float32)
        fields = [F0] + CIN
        inp = {'embedded_features': x}
        for i in range(len(CIN)):
            cin = F0 * fields[i]
            cout = fields[i + 1]
            kw = jax.random.fold_in(ks[1], i)
            inp[f'W{i}'] = jax.random.normal(kw, (cout, cin), dtype=jnp.float32) / np.sqrt(cin)
            inp[f'b{i}'] = jnp.zeros((cout,), dtype=jnp.float32)
        return inp
    _L0_rec_all = _L0_rec_setup()
    _L0_rec_in = {k: v for k, v in _L0_rec_all.items() if k in ('W0', 'b0', 'W1', 'b1', 'W2', 'b2')}
    del _L0_rec_all
    return {'dense_ctx': dense_ctx, 'ids': ids, 'tbl_0': tbl_0, 'tbl_1': tbl_1, 'tbl_2': tbl_2, 'tbl_3': tbl_3, 'tbl_4': tbl_4, 'tbl_5': tbl_5, 'tbl_6': tbl_6, 'tbl_7': tbl_7, 'tbl_8': tbl_8, 'tbl_9': tbl_9, 'tbl_10': tbl_10, 'tbl_11': tbl_11, 'tbl_12': tbl_12, 'tbl_13': tbl_13, 'tbl_14': tbl_14, 'tbl_15': tbl_15, 'tbl_16': tbl_16, 'tbl_17': tbl_17, 'tbl_18': tbl_18, 'tbl_19': tbl_19, 'tbl_20': tbl_20, 'tbl_21': tbl_21, 'tbl_22': tbl_22, 'tbl_23': tbl_23, 'tbl_24': tbl_24, 'tbl_25': tbl_25, 'tbl_26': tbl_26, 'tbl_27': tbl_27, 'tbl_28': tbl_28, 'tbl_29': tbl_29, 'tbl_30': tbl_30, 'tbl_31': tbl_31, 'tbl_32': tbl_32, 'tbl_33': tbl_33, 'tbl_34': tbl_34, 'tbl_35': tbl_35, 'tbl_36': tbl_36, 'tbl_37': tbl_37, 'tbl_38': tbl_38, 'W_top1': W_top1, 'b_top1': b_top1, 'W_top2': W_top2, 'b_top2': b_top2, 'W_top3': W_top3, 'L0_rec_W0': _L0_rec_in['W0'], 'L0_rec_b0': _L0_rec_in['b0'], 'L0_rec_W1': _L0_rec_in['W1'], 'L0_rec_b1': _L0_rec_in['b1'], 'L0_rec_W2': _L0_rec_in['W2'], 'L0_rec_b2': _L0_rec_in['b2']}

def reference(dense_ctx, ids, tbl_0, tbl_1, tbl_2, tbl_3, tbl_4, tbl_5, tbl_6, tbl_7, tbl_8, tbl_9, tbl_10, tbl_11, tbl_12, tbl_13, tbl_14, tbl_15, tbl_16, tbl_17, tbl_18, tbl_19, tbl_20, tbl_21, tbl_22, tbl_23, tbl_24, tbl_25, tbl_26, tbl_27, tbl_28, tbl_29, tbl_30, tbl_31, tbl_32, tbl_33, tbl_34, tbl_35, tbl_36, tbl_37, tbl_38, W_top1, b_top1, W_top2, b_top2, W_top3, L0_rec_W0, L0_rec_b0, L0_rec_W1, L0_rec_b1, L0_rec_W2, L0_rec_b2):
    import jax
    import jax.numpy as jnp

    def _L0_rec_ref(embedded_features, W0, b0, W1, b1, W2, b2):
        import jax, jax.numpy as jnp
        import numpy as np
        B, F0, D = (512, 39, 16)
        CIN = [128, 128, 128]

        def _cin_layer(X0, Xi, W, b):
            H = W.shape[0]
            F0_, Fi = (X0.shape[1], Xi.shape[1])
            Wr = W.reshape(H, F0_, Fi)
            return jnp.einsum('hjk,bjd,bkd->bhd', Wr, X0, Xi) + b[None, :, None]
        X0 = embedded_features
        Ws = [(W0, b0), (W1, b1), (W2, b2)]
        Xi = X0
        res = []
        for W, b in Ws:
            Xi = _cin_layer(X0, Xi, W, b)
            res.append(Xi.sum(axis=2))
        return jnp.concatenate(res, axis=1)
    e = jnp.stack([tbl_0[ids[:, 0]], tbl_1[ids[:, 1]], tbl_2[ids[:, 2]], tbl_3[ids[:, 3]], tbl_4[ids[:, 4]], tbl_5[ids[:, 5]], tbl_6[ids[:, 6]], tbl_7[ids[:, 7]], tbl_8[ids[:, 8]], tbl_9[ids[:, 9]], tbl_10[ids[:, 10]], tbl_11[ids[:, 11]], tbl_12[ids[:, 12]], tbl_13[ids[:, 13]], tbl_14[ids[:, 14]], tbl_15[ids[:, 15]], tbl_16[ids[:, 16]], tbl_17[ids[:, 17]], tbl_18[ids[:, 18]], tbl_19[ids[:, 19]], tbl_20[ids[:, 20]], tbl_21[ids[:, 21]], tbl_22[ids[:, 22]], tbl_23[ids[:, 23]], tbl_24[ids[:, 24]], tbl_25[ids[:, 25]], tbl_26[ids[:, 26]], tbl_27[ids[:, 27]], tbl_28[ids[:, 28]], tbl_29[ids[:, 29]], tbl_30[ids[:, 30]], tbl_31[ids[:, 31]], tbl_32[ids[:, 32]], tbl_33[ids[:, 33]], tbl_34[ids[:, 34]], tbl_35[ids[:, 35]], tbl_36[ids[:, 36]], tbl_37[ids[:, 37]], tbl_38[ids[:, 38]]], axis=1)
    z = _L0_rec_ref(e, L0_rec_W0, L0_rec_b0, L0_rec_W1, L0_rec_b1, L0_rec_W2, L0_rec_b2)
    z = z.reshape(z.shape[0], -1)
    h = jnp.concatenate([z, dense_ctx], axis=1)
    h = jnp.maximum(h @ W_top1 + b_top1, 0.0)
    h = jnp.maximum(h @ W_top2 + b_top2, 0.0)
    y = h @ W_top3
    return y

_drawn_inputs = setup_inputs


def setup_inputs(seed=0):
    import zlib

    import numpy as np

    out = dict(_drawn_inputs(seed))
    spreads = {'b_top1': (0.0, 0.1),
     'b_top2': (0.0, 0.1),
     'L0_rec_b0': (0.0, 0.1),
     'L0_rec_b1': (0.0, 0.1),
     'L0_rec_b2': (0.0, 0.1)}
    factors = {'tbl_0': 8.0,
     'tbl_1': 5.892,
     'tbl_2': 5.36,
     'tbl_3': 7.012,
     'tbl_4': 8.0,
     'tbl_5': 8.0,
     'tbl_6': 8.0,
     'tbl_7': 7.14,
     'tbl_8': 8.0,
     'tbl_9': 8.0,
     'tbl_10': 8.0,
     'tbl_11': 6.557,
     'tbl_12': 8.0,
     'tbl_13': 8.0,
     'tbl_14': 4.249,
     'tbl_15': 5.429,
     'tbl_16': 8.0,
     'tbl_17': 8.0,
     'tbl_18': 8.0,
     'tbl_19': 5.96,
     'tbl_20': 7.099,
     'tbl_21': 8.0,
     'tbl_22': 8.0,
     'tbl_23': 8.0,
     'tbl_24': 8.0,
     'tbl_25': 7.236,
     'tbl_26': 5.872,
     'tbl_27': 8.0,
     'tbl_28': 8.0,
     'tbl_29': 8.0,
     'tbl_30': 6.802,
     'tbl_31': 6.534,
     'tbl_32': 8.0,
     'tbl_33': 6.878,
     'tbl_34': 8.0,
     'tbl_35': 7.4,
     'tbl_36': 8.0,
     'tbl_37': 6.909,
     'tbl_38': 8.0,
     'L0_rec_W0': 3.179}
    for name, (base, spread) in spreads.items():
        noise = np.random.default_rng([zlib.crc32(name.encode()), seed]).standard_normal(out[name].shape)
        drawn = base * np.exp(spread * noise) if base else spread * noise
        out[name] = jnp.asarray(drawn.astype(out[name].dtype))
    for name, factor in factors.items():
        out[name] = (out[name] * factor).astype(out[name].dtype)
    return out
```

```python
from contextlib import ExitStack

import concourse.bass as bass
from concourse import mybir

F32 = mybir.dt.float32
F32R = mybir.dt.float32r
I32 = mybir.dt.int32
U32 = mybir.dt.uint32
ALU = mybir.AluOpType
ACT = mybir.ActivationFunctionType
AX = mybir.AxisListType

P = 128
B, NF, D, H = 512, 39, 16, 128
CH = B // P
SPC = 4
STEPS = CH * SPC
N = B * D // STEPS
BS = N // D
JL, KL = 8, 16
NJ = 5
NK0 = 3
NK1 = H // KL
ROWS_X0 = NK0 * KL
JLAST = NF - (NJ - 1) * JL
GB = P // D
GRP = N // P
NG = NF + 1

L0_TILES = [(0, 0, 0), (1, 0, 0), (0, 1, 1), (1, 1, 1), (2, 1, 0), (3, 1, 0), (4, 0, 1), (4, 1, 1), (4, 2, 0)]
L0_UNITS = [(0, 2), (2, 2), (4, 2), (6, 2), (8, 1)]

SPLIT_J = (0, 2, 3)
L1_UNITS = [(J, K) for half in (0, 4) for K in (half, half + 2) for J in range(NJ)]
HALF = len(L1_UNITS) // 2

UNITS = ([("L1", u) for u in L1_UNITS[:HALF]] + [("L0", u) for u in L0_UNITS] +
         [("L1", u) for u in L1_UNITS[HALF:]])
NU = len(UNITS)
L0_AT = HALF
L0_END = HALF + len(L0_UNITS)


def is_split(i):
    kind, u = UNITS[i]
    return kind == "L1" and u[0] in SPLIT_J


SPLIT_PER_STEP = sum(is_split(i) for i in range(NU))
WHOLE_PER_STEP = NU - SPLIT_PER_STEP
RING_W = 4
RING_S = 3
assert SPC * SPLIT_PER_STEP % RING_S == 0 and SPC * WHOLE_PER_STEP % RING_W == 0


class Step:

    def __init__(self, c, q, has_next=True):
        self.c, self.q, self.has_next = c, q, has_next
        self.static = isinstance(c, int)

    def count(self, per_step, const):
        return self.c * (SPC * per_step) + (per_step * self.q + const)

    def units(self):
        if self.q == -1 and self.static and self.c == 0:
            return list(range(L0_AT, L0_END))
        if not self.has_next:
            return list(range(L0_AT)) + list(range(L0_END, NU))
        return list(range(NU))

    def place(self, i, split):
        before = sum(is_split(u) == split for u in self.units() if u < i)
        if self.q == -1:
            return before, before
        per = SPLIT_PER_STEP if split else WHOLE_PER_STEP
        const = before + sum(is_split(u) == split for u in range(L0_AT, L0_END))
        return self.count(per, const), per * self.q + const

    def done(self, i, split):
        per = SPLIT_PER_STEP if split else WHOLE_PER_STEP
        first = sum(is_split(u) == split for u in range(L0_AT, L0_END))
        upto = sum(is_split(u) == split for u in self.units() if u <= i)
        if self.q == -1:
            return upto
        return self.count(per, first + upto)


def wait(eng, sem, value):
    if isinstance(value, int) and value <= 0:
        return
    eng.wait_ge(sem, value)


def build(nc, dense_ctx, ids, tables, w_top1, b_top1, w_top2, b_top2, w_top3, w0, b0, w1, b1, w2, b2,
          ident_in, mask_in, out):
    ctx = ExitStack()
    with ctx:
        def sb(name, shape, dt=F32):
            return ctx.enter_context(nc.sbuf_tensor(name, shape, dt))

        def ps(name):
            return ctx.enter_context(nc.psum_tensor(name, [P, 512], F32))

        def sem(name):
            return ctx.enter_context(nc.semaphore(name))

        x0_dram = nc.dram_tensor("x0_scratch", [ROWS_X0, B * D], F32).ap()
        x1_dram = nc.dram_tensor("x1_scratch", [STEPS, H, N], F32).ap()

        l1_tiles = [(J, K + m) for (J, K) in L1_UNITS for m in range(2)]
        l1_split = [t for t in l1_tiles if t[0] in SPLIT_J]
        l1_whole = [t for t in l1_tiles if t[0] not in SPLIT_J]
        w1_head = sb("w1_head", [P, len(l1_split), H], F32R)
        w1_tail = sb("w1_tail", [P, len(l1_split), H], F32R)
        w1_whole = sb("w1_whole", [P, len(l1_whole), H])
        w0_tiles = sb("w0_tiles", [P, len(L0_TILES), H])
        w2_tiles = sb("w2_tiles", [P, NF, H])
        ident = sb("ident", [P, P])
        mask = sb("mask", [P, GB])
        bias = sb("bias", [P, 3])
        bias16 = sb("bias16", [P, 1])
        bias_top = sb("bias_top", [P, 6])
        wt3 = sb("wt3", [P, 2])
        dense = sb("dense", [P, CH, 16])
        dense_t = sb("dense_t", [16, B])

        g_sum = sb("g_sum", [P, NG, P])
        raw = g_sum[:, 0:NF, :].rearrange("p a b -> p (a b)")

        rep_j = sb("rep_j", [P, 2, NJ, N])
        rep_k = sb("rep_k", [P, NK0, N])
        rep_x1 = sb("rep_x1", [P, NK1, N])
        z_whole = sb("z_whole", [P, RING_W, 2, N])
        z_bytes = z_whole[:].rearrange("p r t n -> p (r t n)")
        w0_raw = z_bytes[:, 0:NF * NF]
        w0_sym = z_bytes[:, 2048:2048 + len(L0_TILES) * P].rearrange(
            "p (t j k) -> p t j k", t=len(L0_TILES), j=JL)
        z_full = sb("z_full", [P, RING_S, 2, N])
        z_head = sb("z_head", [P, RING_S, 2, N], F32R)
        z_tail = sb("z_tail", [P, RING_S, 2, N], F32R)

        idx = sb("idx", [P, NF], I32)
        emb = sb("emb", [P, NF, D])
        x0_sb = sb("x0_sb", [P, P * D])
        x0_p = sb("x0_p", [P, CH * GRP, NF])
        x0_blk = sb("x0_blk", [P, GRP, NG, GB])
        x1_sb = sb("x1_sb", [P, N])
        x2_sb = sb("x2_sb", [P, N])
        x2_p = sb("x2_p", [P, GRP, H])
        z0 = sb("z0", [P, B])
        z1 = sb("z1", [P, B])
        z2 = sb("z2", [P, B])
        wt1 = rep_j[:, 0, 0:4, :]
        wt2 = rep_k[:].rearrange("p a n -> p (a n)")[:, 0:4 * 256].rearrange("p (t m) -> p t m", t=4)
        h1 = rep_x1[:, 0:4, :]
        h2 = rep_x1[:, 4:6, :]
        y_sb = sb("y_sb", [1, B])

        acc1 = [ps("acc1_even"), ps("acc1_odd")]
        acc0 = ps("acc0")
        turn_x2_ps = ps("turn_x2")
        turn_x0 = ps("turn_x0")
        g_ps = [ps("g_even"), ps("g_odd")]
        z2_ps = ps("z2_ps")

        ld_const, ld_w0, ld_w1, ld_w2, ld_top = sem("ld_const"), sem("ld_w0"), sem("ld_w1"), sem("ld_w2"), sem("ld_top")
        ld_dense = sem("ld_dense")
        ld_idx, gathered = sem("ld_idx"), sem("gathered")
        x0_stored, x1_stored = sem("x0_stored"), sem("x1_stored")
        ld_rep_j, ld_rep_k, ld_x1_a, ld_x1_b = sem("ld_rep_j"), sem("ld_rep_k"), sem("ld_x1_a"), sem("ld_x1_b")
        out_stored = sem("out_stored")
        sp_passed, pe_passed, pool_passed = sem("sp_passed"), sem("pe_passed"), sem("pool_passed")
        w0_staged, w0_zeroed, w_turned, w_copied, w_tailed = (sem("w0_staged"), sem("w0_zeroed"), sem("w_turned"),
                                                              sem("w_copied"), sem("w_tailed"))
        b2_scaled = sem("b2_scaled")
        whole_ready, whole_used = sem("whole_ready"), sem("whole_used")
        full_ready, head_ready, tail_ready, split_used = (sem("full_ready"), sem("head_ready"), sem("tail_ready"),
                                                          sem("split_used"))
        x1_made, x2_made, z0_made = sem("x1_made"), sem("x2_made"), sem("z0_made")
        emb_turned, x0_made, x0_zeroed, x0_turned, x0p_made = (sem("emb_turned"), sem("x0_made"), sem("x0_zeroed"),
                                                               sem("x0_turned"), sem("x0p_made"))
        blk_ones, blk_made, x2_turned, x2p_made = sem("blk_ones"), sem("blk_made"), sem("x2_turned"), sem("x2p_made")
        g_summed, g_made, z1_made, z2_summed, z2_made = (sem("g_summed"), sem("g_made"), sem("z1_made"),
                                                         sem("z2_summed"), sem("z2_made"))
        dense_turned, dense_made = sem("dense_turned"), sem("dense_made")
        h1_summed, h1_made, h2_summed, h2_made, y_summed, y_made = (
            sem("h1_summed"), sem("h1_made"), sem("h2_summed"), sem("h2_made"), sem("y_summed"), sem("y_made"))

        w1_view = raw.rearrange("h (j k) -> h j k", j=NF).rearrange("h j (l g) -> h j l g", g=NK1)
        turns = []

        def w1_source(J, K):
            return w1_view[:, J * JL:min(J * JL + JL, NF), :, K]

        for a in range(0, len(L0_TILES), 4):
            ts = list(range(a, min(a + 4, len(L0_TILES))))
            turns.append(([w0_sym[:, t].rearrange("p j k -> p (j k)") for t in ts], P, "w0", a))
        for kind, tiles in (("split", l1_split), ("whole", l1_whole)):
            a = 0
            while a < len(tiles):
                rows = JLAST * KL if tiles[a][0] == NJ - 1 else P
                b_ = a
                while b_ < len(tiles) and b_ - a < 4 and (tiles[b_][0] == NJ - 1) == (rows < P):
                    b_ += 1
                turns.append(([w1_source(*t) for t in tiles[a:b_]], rows, kind, a))
                a = b_
        last_w1_turn = len(turns)
        for a in range(0, NF, 4):
            js = list(range(a, min(a + 4, NF)))
            turns.append(([raw[:, j * H:(j + 1) * H] for j in js], P, "w2", a))
        turn_bank = [turn_x2_ps, g_ps[0], g_ps[1], z2_ps]
        splits_upto = [sum(t[2] == "split" for t in turns[:g + 1]) for g in range(len(turns))]

        def turn_dst(kind, rows, a, n):
            dst = {"w0": w0_tiles, "split": w1_head, "whole": w1_whole, "w2": w2_tiles}[kind]
            return dst[0:rows, a:a + n, :]

        PE_TURN_X2, PE_G = 5, (9, 16)
        PE_EMB = (3, 8, 13, 18)
        PE_X0P = (9, 13, 17, 21)
        PE_Z2 = 21
        DVE_SUM_X1 = 21
        LAG = 2

        def used(eng, st, i):
            wait(eng, split_used if is_split(i) else whole_used, st.done(i, is_split(i)))

        def k_rows(J):
            return JLAST * KL if J == NJ - 1 else P

        block = ctx.enter_context(nc.Block())

        @block.sync
        def _(sp):
            def settle():
                sp.sem_inc(sp_passed, 1)

            sp.dma_start(ident[:], ident_in).then_inc(ld_const, 16)
            sp.dma_start(mask[:], mask_in).then_inc(ld_const, 16)
            for i, b_ in enumerate((b0, b1, b2)):
                sp.dma_start(bias[:, i:i + 1], b_.rearrange("(p o) -> p o", o=1)).then_inc(ld_const, 16)
            sp.dma_start(w0_raw, w0).then_inc(ld_w0, 16)
            sp.dma_start(raw, w1).then_inc(ld_w1, 16)

            def store_x0(c):
                sp.wait_ge(x0_made, c * 4 + 4)
                settle()
                sp.dma_start(x0_dram[:, bass.ds(c * (P * D), P * D)], x0_sb[0:ROWS_X0, :]).then_inc(x0_stored, 16)

            def load_rep(st, q):
                settle()
                cols = bass.ds(st.count(N, 0), N)
                for J in range(NJ):
                    src = x0_dram[J * JL:(J + 1) * JL, cols].unsqueeze(1).to_broadcast([JL, KL, N])
                    sp.dma_start(rep_j[:, q % 2, J], src).then_inc(ld_rep_j, 16)
                for K in range(NK0):
                    src = x0_dram[K * KL:(K + 1) * KL, cols].unsqueeze(0).to_broadcast([JL, KL, N])
                    sp.dma_start(rep_k[:, K], src).then_inc(ld_rep_k, 16)

            def mults_done(st, i):
                settle()
                wait(sp, whole_ready, st.done(i, False))
                settle()
                if SPLIT_PER_STEP:
                    wait(sp, full_ready, st.done(i, True))
                    settle()

            def load_x1(st, half, semaphore):
                settle()
                src = x1_dram[bass.ds(st.count(1, 0), 1)].rearrange("s (l g) n -> (s l) g n", g=NK1)
                src = src[:, half * 4:half * 4 + 4, :].rearrange("l g n -> l (g n)").unsqueeze(0).to_broadcast([JL, KL, 4 * N])
                sp.dma_start(rep_x1[:, half * 4:half * 4 + 4, :], src).then_inc(semaphore, 16)

            def store_x1(st):
                wait(sp, x1_made, st.count(1, 1))
                settle()
                dst = x1_dram[bass.ds(st.count(1, 0), 1)].rearrange("s k n -> (s k) n")
                sp.dma_start(dst, x1_sb[:]).then_inc(x1_stored, 16)
                wait(sp, x1_stored, st.count(16, 16))
                settle()

            for t in range(2):
                sp.dma_start(wt3[:, t:t + 1], w_top3[t * P:(t + 1) * P]).then_inc(ld_dense, 16)
            for t in range(6):
                b_ = b_top1[t * P:(t + 1) * P] if t < 4 else b_top2[(t - 4) * P:(t - 3) * P]
                sp.dma_start(bias_top[:, t:t + 1], b_.rearrange("(p o) -> p o", o=1)).then_inc(ld_dense, 16)
            sp.dma_start(dense[:], dense_ctx.rearrange("(c p) f -> p c f", p=P)).then_inc(ld_dense, 16)
            sp.wait_ge(w_turned, last_w1_turn)
            sp.dma_start(raw, w2).then_inc(ld_w2, 16)

            store_x0(0)
            sp.wait_ge(x0_stored, 16)
            load_rep(Step(0, 0), 0)
            store_x1(Step(0, 0))
            load_x1(Step(0, 0), 0, ld_x1_a)
            def step(c, q, has_next=True, chunk_after=False):
                st, prev, nxt = Step(c, q, has_next), Step(c, q - 1), Step(c, q + 1)
                mults_done(prev, NU - 1)
                load_x1(st, 1, ld_x1_b)
                if not has_next:
                    sp.dma_start(wt1[:, 0:3, :], w_top1[0:3 * P].rearrange("(t p) m -> p t m", p=P)).then_inc(ld_top, 16)
                    sp.dma_start(wt1[0:16, 3, :], w_top1[3 * P:3 * P + 16]).then_inc(ld_top, 16)
                    sp.dma_start(wt2, w_top2.rearrange("(t p) m -> p t m", p=P)).then_inc(ld_top, 16)
                    return
                if q == 3 and chunk_after:
                    wait(sp, x0_stored, c * 16 + 32)
                load_rep(nxt, q + 1)
                store_x1(nxt)
                mults_done(st, L0_AT - 1)
                load_x1(nxt, 0, ld_x1_a)
                if q == 2 and chunk_after:
                    store_x0(c + 1)

            step(0, 0)
            step(0, 1)
            with sp.Fori(0, CH - 1) as c:
                for q in range(2, 6):
                    step(c, q, chunk_after=True)
            for q in range(2, 4):
                step(CH - 1, q, has_next=q < 3)
            sp.wait_ge(y_made, 1)
            sp.dma_start(out.rearrange("b o -> o b"), y_sb[:]).then_inc(out_stored, 16)
            sp.wait_ge(out_stored, 16)

        @block.gpsimd
        def _(pool):
            nc.gpsimd.memset(x0_sb[:], 0.0).then_inc(x0_zeroed, 1)

            def gather(c):
                if not (isinstance(c, int) and c == 0):
                    pool.wait_ge(gathered, c * (16 * NF))
                pool.dma_start(idx[:], ids[bass.ds(c * P, P), :]).then_inc(ld_idx, 16)
                pool.wait_ge(ld_idx, c * 16 + 16)
                if not (isinstance(c, int) and c == 0):
                    pool.wait_ge(emb_turned, c * 4)
                pool.sem_inc(pool_passed, 1)
                for f in range(NF):
                    pool.indirect_dma_start(
                        out=emb[:, f, :], out_offset=None, in_=tables[f],
                        in_offset=bass.IndirectOffsetOnAxis(ap=idx[:, f:f + 1].bitcast(U32), axis=0)
                    ).then_inc(gathered, 16)

            gather(0)
            with pool.Fori(1, CH) as c:
                gather(c)

        @block.tensor
        def _(pe):
            turned = [0]

            def turn_weights(g):
                srcs, rows, kind, _ = turns[g]
                if g >= len(turn_bank):
                    old = g - len(turn_bank)
                    pe.wait_ge(w_copied, old + 1)
                    wait(pe, w_tailed, splits_upto[old])
                for m, src in enumerate(srcs):
                    mm = pe.transpose(turn_bank[g % len(turn_bank)][0:rows, m * P:(m + 1) * P], src, ident[:])
                mm.then_inc(w_turned, 1)

            def turn_emb(c, part):
                if part == 0:
                    pe.wait_ge(gathered, c * (16 * NF) + 16 * NF)
                    wait(pe, x0p_made, c * 4)
                wait(pe, x0_made, c * 4 + part)
                pe.sem_inc(pe_passed, 1)
                for m in range(4):
                    mm = pe.transpose(turn_x0[0:NF, m * P:(m + 1) * P], emb[:, :, 4 * part + m], ident[:])
                mm.then_inc(emb_turned, 1)

            def turn_x0p(c, part):
                if part == 0:
                    pe.wait_ge(x0_made, c * 4 + 4)
                wait(pe, x0p_made, c * 4 + part)
                for m in range(GRP):
                    g = part * GRP + m
                    mm = pe.transpose(turn_x0[:, m * P:(m + 1) * P], x0_sb[:, g * P:(g + 1) * P], ident[:])
                mm.then_inc(x0_turned, 1)

            def unit(st, i):
                kind, u = UNITS[i]
                split = is_split(i)
                count, at = st.place(i, split)
                slot = at % (RING_S if split else RING_W)
                wait(pe, tail_ready if split else whole_ready, count + 1)
                if kind == "L0":
                    tiles = [(w0_tiles[:, t], P, t == 0, t == len(L0_TILES) - 1) for t in range(u[0], u[0] + u[1])]
                    acc = acc0
                    if i == L0_AT:
                        wait(pe, x1_made, st.count(1, 1))
                else:
                    J, K = u
                    tiles = []
                    for m in range(2):
                        r, first = k_rows(J), i == 0 and m == 0
                        last = i == NU - 1 and m == 1
                        if split:
                            n = l1_split.index((J, K + m))
                            tiles.append(((w1_head[0:r, n], w1_tail[0:r, n]), r, first, last))
                        else:
                            tiles.append((w1_whole[0:r, l1_whole.index((J, K + m))], r, first, last))
                    acc = acc1[st.q % 2]
                    if i == 0:
                        wait(pe, x2_made, st.count(1, -1))
                for m, (w, r, first, last) in enumerate(tiles):
                    if split:
                        head, tail = z_head[0:r, slot, m], z_tail[0:r, slot, m]
                        pe.matmul(acc[:], w[0], head, start=first, stop=False)
                        pe.matmul(acc[:], w[0], tail, start=False, stop=False)
                        mm = pe.matmul(acc[:], w[1], head, start=False, stop=last)
                    else:
                        mm = pe.matmul(acc[:], w, z_whole[0:r, slot, m], start=first, stop=last)
                mm.then_inc(split_used if split else whole_used, 1)

            def turn_x2(st):
                wait(pe, x2_made, st.count(1, 1))
                wait(pe, x2p_made, st.count(1, 0))
                for g in range(GRP):
                    mm = pe.transpose(turn_x2_ps[:, g * P:(g + 1) * P], x2_sb[:, g * P:(g + 1) * P], ident[:])
                mm.then_inc(x2_turned, 1)

            def g_products(st, groups):
                if groups[0] == 0:
                    wait(pe, x2p_made, st.count(1, 1))
                    wait(pe, blk_made, st.count(1, 1))
                for g in groups:
                    if g >= 2:
                        pe.wait_ge(g_made, st.count(GRP, g - 1))
                    pe.matmul(g_ps[g % 2][:, 0:NG * GB], x2_p[:, g], x0_blk[:, g].rearrange("p j b -> p (j b)"),
                              start=True, stop=True).then_inc(g_summed, 1)

            def l2_product(c):
                wait(pe, g_made, c * (GRP * SPC) + GRP * SPC)
                for j in range(NF):
                    mm = pe.matmul(z2_ps[:, 0:P], w2_tiles[:, j], g_sum[:, j, :], start=j == 0, stop=j == NF - 1)
                mm.then_inc(z2_summed, 1)

            def step(c, q, has_next=True, chunk_next=None):
                st, prev = Step(c, q, has_next), Step(c, q - 1)
                for i in st.units():
                    if not (st.static and c * SPC + q == 0):
                        if i == PE_TURN_X2:
                            turn_x2(prev)
                        if i in PE_G:
                            g_products(prev, (0, 1) if i == PE_G[0] else (2, 3))
                    if q == 2 and chunk_next is not None and i in PE_EMB:
                        turn_emb(chunk_next, PE_EMB.index(i))
                    if q == 4 and i in PE_X0P:
                        turn_x0p(chunk_next, PE_X0P.index(i))
                    if q == 4 and i == PE_Z2:
                        l2_product(c)
                    unit(st, i)

            pe.wait_ge(ld_const, 16 * 5)
            pe.wait_ge(w0_staged, len(L0_TILES))
            for g in range(last_w1_turn):
                if turns[g][2] != "w0":
                    pe.wait_ge(ld_w1, 16)
                turn_weights(g)
            for part in range(4):
                turn_emb(0, part)
            for part in range(SPC):
                turn_x0p(0, part)
            pe.wait_ge(ld_dense, 16 * 9)
            for m in range(CH):
                mm = pe.transpose(acc0[0:16, m * P:(m + 1) * P], dense[:, m], ident[:])
            mm.then_inc(dense_turned, 1)
            pe.wait_ge(ld_w2, 16)
            for g in range(last_w1_turn, len(turns)):
                turn_weights(g)
            pe.wait_ge(dense_made, 1)
            pe.wait_ge(w_copied, len(turns))
            wait(pe, w_tailed, splits_upto[-1])
            first = Step(0, -1)
            for i in first.units():
                unit(first, i)
            step(0, 0)
            step(0, 1)
            with pe.Fori(0, CH - 1) as c:
                for q in range(2, 6):
                    step(c, q, chunk_next=c + 1)
            for q in range(2, 4):
                step(CH - 1, q, has_next=q < 3)
            last = Step(CH - 1, 3, False)
            turn_x2(last)
            g_products(last, (0, 1))
            g_products(last, (2, 3))

            l2_product(CH - 1)
            pe.wait_ge(ld_top, 16 * 3)
            pe.wait_ge(z1_made, CH)
            pe.wait_ge(z0_made, STEPS)
            banks = [acc1[0], acc1[1], acc0, turn_x2_ps]
            for m in range(4):
                cols = slice(m * P, (m + 1) * P)
                pe.matmul(banks[m][:], wt1[0:16, 3, cols], dense_t[:], start=True, stop=False)
                pe.matmul(banks[m][:], wt1[:, 0, cols], z0[:], start=False, stop=False)
                pe.matmul(banks[m][:], wt1[:, 1, cols], z1[:], start=False, stop=False)
            pe.wait_ge(z2_made, CH)
            for m in range(4):
                cols = slice(m * P, (m + 1) * P)
                pe.matmul(banks[m][:], wt1[:, 2, cols], z2[:], start=False, stop=True).then_inc(h1_summed, 1)
            for t in range(4):
                pe.wait_ge(h1_made, t + 1)
                for m in range(2):
                    mm = pe.matmul(g_ps[m][:], wt2[:, t, m * P:(m + 1) * P], h1[:, t], start=t == 0, stop=t == 3)
                    if t == 3:
                        mm.then_inc(h2_summed, 1)
            for t in range(2):
                pe.wait_ge(h2_made, t + 1)
                mm = pe.matmul(turn_x0[0:1, :], wt3[:, t:t + 1], h2[:, t], start=t == 0, stop=t == 1)
            mm.then_inc(y_summed, 1)

        @block.vector
        def _(dve):
            nc.vector.memset(w0_sym, 0.0).then_inc(w0_zeroed, 1)
            dve.wait_ge(w0_zeroed, 1)
            dve.wait_ge(ld_w0, 16)
            w0_jk = w0_raw.rearrange("h (j k) -> h j k", j=NF)
            for t, (J, K, both) in enumerate(L0_TILES):
                js, ks = slice(J * JL, min(J * JL + JL, NF)), slice(K * KL, min(K * KL + KL, NF))
                dst = w0_sym[:, t, 0:js.stop - js.start, 0:ks.stop - ks.start]
                if both:
                    ins = nc.vector.tensor_tensor(dst, w0_jk[:, js, ks], w0_jk[:, ks, js].rearrange("h k j -> h j k"),
                                                  ALU.add)
                else:
                    ins = nc.vector.tensor_copy(dst, w0_jk[:, js, ks])
                ins.then_inc(w0_staged, 1)
            dve.wait_ge(ld_const, 16 * 5)
            nc.vector.tensor_scalar(bias16[:], bias[:, 2:3], float(D), None, ALU.mult).then_inc(b2_scaled, 1)
            for g in range(GRP):
                nc.vector.tensor_copy(x0_blk[:, g, NF, :], mask[:]).then_inc(blk_ones, 1)
            n = 0
            for g, (srcs, rows, kind, a) in enumerate(turns):
                if kind == "split":
                    dve.wait_ge(w_copied, g + 1)
                    m = len(srcs)
                    nc.vector.tensor_tensor(
                        w1_tail[0:rows, a:a + m], turn_bank[g % len(turn_bank)][0:rows, 0:m * P].rearrange(
                            "p (t h) -> p t h", t=m),
                        w1_head[0:rows, a:a + m].bitcast(F32), ALU.subtract).then_inc(w_tailed, 1)

            def operands(st, i):
                kind, u = UNITS[i]
                if kind == "L0":
                    slot = (st.q + 1) % 2
                    tiles = L0_TILES[u[0]:u[0] + u[1]]
                    J, K = tiles[0][0], tiles[0][1]
                    if len(tiles) == 1:
                        return rep_j[:, slot, J:J + 1], rep_k[:, K:K + 1]
                    if tiles[1][0] > J:
                        return rep_j[:, slot, J:J + 2], rep_k[:, K:K + 1].to_broadcast([P, 2, N])
                    return rep_j[:, slot, J:J + 1].to_broadcast([P, 2, N]), rep_k[:, K:K + 2]
                J, K = u
                return rep_j[:, st.q % 2, J:J + 1].to_broadcast([P, 2, N]), rep_x1[:, K:K + 2]

            def tail(st, i):
                count, at = st.place(i, True)
                slot = at % RING_S
                dve.wait_ge(head_ready, count + 1)
                wait(dve, split_used, count + (1 - RING_S))
                nc.vector.tensor_tensor(z_tail[:, slot], z_full[:, slot],
                                        z_head[:, slot].bitcast(F32), ALU.subtract).then_inc(tail_ready, 1)

            def product(st, i):
                split = is_split(i)
                count, at = st.place(i, split)
                slot = at % (RING_S if split else RING_W)
                if i == L0_AT:
                    dve.wait_ge(ld_rep_j, st.count(16 * NJ, 32 * NJ))
                    dve.wait_ge(ld_rep_k, st.count(16 * NK0, 32 * NK0))
                if i == 0:
                    dve.wait_ge(ld_x1_a, st.count(16, 16))
                if i == L0_END:
                    dve.wait_ge(ld_x1_b, st.count(16, 16))
                in0, in1 = operands(st, i)
                tiles = in0.shape[1]
                if split:
                    wait(dve, tail_ready, count + (1 - RING_S))
                    nc.vector.tensor_tensor(z_full[:, slot], in0, in1, ALU.mult).then_inc(full_ready, 1)
                else:
                    wait(dve, whole_used, count + (1 - RING_W))
                    nc.vector.tensor_tensor(z_whole[:, slot, 0:tiles], in0, in1, ALU.mult).then_inc(whole_ready, 1)

            def sum_x1(st):
                dve.wait_ge(x1_made, st.count(1, 1))
                nc.vector.tensor_reduce(z0[:, bass.ds(st.count(BS, 0), BS)], x1_sb[:].rearrange("p (b d) -> p b d", d=D),
                                        AX.X, ALU.add).then_inc(z0_made, 1)

            def step(c, q, has_next=True):
                st = Step(c, q, has_next)
                late = None
                for i in st.units():
                    product(st, i)
                    if late is not None:
                        tail(st, late)
                    late = i if is_split(i) else None
                    if i == DVE_SUM_X1 and has_next and q >= 0:
                        sum_x1(Step(c, q + 1))

            dve.wait_ge(w_turned, sum(t[2] == "w0" for t in turns))
            step(0, -1)
            sum_x1(Step(0, 0))
            step(0, 0)
            step(0, 1)
            with dve.Fori(0, CH - 1) as c:
                for q in range(2, 6):
                    step(c, q)
            for q in range(2, 4):
                step(CH - 1, q, has_next=q < 3)

        @block.scalar
        def _(act):
            act.wait_ge(ld_const, 16 * 5)

            def copy_turned(g):
                srcs, rows, kind, a = turns[g]
                act.wait_ge(w_turned, g + 1)
                m = len(srcs)
                nc.scalar.activation(turn_dst(kind, rows, a, m),
                                     turn_bank[g % len(turn_bank)][0:rows, 0:m * P].rearrange("p (t h) -> p t h", t=m),
                                     ACT.Copy).then_inc(w_copied, 1)

            def copy_emb(c, part):
                if part == 0:
                    wait(act, x0_stored, c * 16)
                    wait(act, x0_turned, c * SPC)
                act.wait_ge(emb_turned, c * 4 + (part + 1))
                dst = x0_sb[0:NF, :].rearrange("j (b d) -> j b d", d=D)[:, :, 4 * part:4 * part + 4]
                nc.scalar.activation(dst.rearrange("j b m -> j m b"),
                                     turn_x0[0:NF, :].rearrange("j (m b) -> j m b", m=4), ACT.Copy).then_inc(x0_made, 1)

            def copy_x0p(c, part):
                act.wait_ge(x0_turned, c * SPC + (part + 1))
                nc.scalar.activation(x0_p[:, part * GRP:(part + 1) * GRP, :],
                                     turn_x0[:].rearrange("p (g j) -> p g j", g=GRP)[:, :, 0:NF],
                                     ACT.Copy).then_inc(x0p_made, 1)

            def make_x1(st):
                used(act, Step(st.c, st.q - 1), L0_END - 1)
                wait(act, x1_stored, st.count(16, 0))
                wait(act, z0_made, st.count(1, 0))
                nc.scalar.activation(x1_sb[:], acc0[:], ACT.Identity, bias=bias[:, 0:1]).then_inc(x1_made, 1)

            def make_x2(st):
                used(act, st, NU - 1)
                wait(act, x2_turned, st.count(1, 0))
                nc.scalar.activation(x2_sb[:], acc1[st.q % 2][:], ACT.Identity, bias=bias[:, 1:2]).then_inc(x2_made, 1)

            def make_blk(st):
                wait(act, g_summed, st.count(GRP, 0))
                part = st.q % SPC
                act.wait_ge(x0p_made, st.count(1, SPC - part))
                for b_ in range(GB):
                    ins = nc.scalar.activation(x0_blk[:, :, 0:NF, b_], x0_p[:, part * GRP:(part + 1) * GRP, :], ACT.Copy,
                                               scale=mask[:, b_:b_ + 1])
                ins.then_inc(blk_made, 1)

            def make_x2p(st):
                act.wait_ge(x2_turned, st.count(1, 1))
                wait(act, g_summed, st.count(GRP, 0))
                nc.scalar.activation(x2_p[:], turn_x2_ps[:].rearrange("p (g h) -> p g h", g=GRP),
                                     ACT.Copy).then_inc(x2p_made, 1)

            def copy_g(st, groups):
                if st.q % SPC == 0 and groups[0] == 0:
                    wait(act, z2_summed, st.c + st.q // SPC)
                for g in groups:
                    act.wait_ge(g_summed, st.count(GRP, g + 1))
                    b_ = (st.q % SPC) * BS + g * GB
                    nc.scalar.activation(g_sum[:, :, b_:b_ + GB],
                                         g_ps[g % 2][:, 0:NG * GB].rearrange("p (j b) -> p j b", b=GB),
                                         ACT.Copy).then_inc(g_made, 1)

            def make_z1(c):
                act.wait_ge(g_made, c * (SPC * GRP) + SPC * GRP)
                nc.scalar.activation(z1[:, bass.ds(c * P, P)], g_sum[:, NF, :], ACT.Copy).then_inc(z1_made, 1)

            def make_z2(c):
                act.wait_ge(z2_summed, c + 1)
                nc.scalar.activation(z2[:, bass.ds(c * P, P)], z2_ps[:, 0:P], ACT.Identity,
                                     bias=bias16[:]).then_inc(z2_made, 1)

            def head(st, i):
                count, at = st.place(i, True)
                slot = at % RING_S
                act.wait_ge(full_ready, count + 1)
                wait(act, split_used, count + (1 - RING_S))
                nc.scalar.activation(z_head[:, slot], z_full[:, slot], ACT.Copy).then_inc(head_ready, 1)

            def step(c, q, has_next=True, chunk_next=None):
                st, prev = Step(c, q, has_next), Step(c, q - 1)
                first = st.static and c * SPC + q == 0
                for i in st.units():
                    if is_split(i):
                        head(st, i)
                    if not first:
                        if i == 2:
                            make_x2(prev)
                        if i == 3:
                            make_blk(prev)
                        if i == PE_TURN_X2 + LAG:
                            make_x2p(prev)
                        if i == PE_G[0] + LAG or (not has_next and i == L0_END):
                            copy_g(prev, (0, 1))
                        if i == PE_G[1] + LAG:
                            copy_g(prev, (2, 3))
                    if q == 2 and chunk_next is not None and i - LAG in PE_EMB:
                        copy_emb(chunk_next, PE_EMB.index(i - LAG))
                    if q == 4 and i - LAG in PE_X0P:
                        copy_x0p(chunk_next, PE_X0P.index(i - LAG))
                    if i == L0_END + LAG and has_next:
                        make_x1(Step(c, q + 1))
                    if q == 4 and i == PE_G[1] + LAG + 1:
                        make_z1(c)
                    if q == 4 and i == PE_Z2 + LAG:
                        make_z2(c)

            for g in range(last_w1_turn):
                copy_turned(g)
            act.wait_ge(x0_zeroed, 1)
            for part in range(4):
                copy_emb(0, part)
            for part in range(SPC):
                copy_x0p(0, part)
            act.wait_ge(dense_turned, 1)
            nc.scalar.activation(dense_t[:], acc0[0:16, :], ACT.Copy).then_inc(dense_made, 1)
            for g in range(last_w1_turn, len(turns)):
                copy_turned(g)
            make_x1(Step(0, 0))
            act.wait_ge(blk_ones, GRP)
            act.wait_ge(b2_scaled, 1)
            step(0, 0)
            step(0, 1)
            with act.Fori(0, CH - 1) as c:
                for q in range(2, 6):
                    step(c, q, chunk_next=c + 1)
            for q in range(2, 4):
                step(CH - 1, q, has_next=q < 3)
            last = Step(CH - 1, 3, False)
            make_x2(last)
            make_blk(last)
            make_x2p(last)
            copy_g(last, (0, 1))
            copy_g(last, (2, 3))
            make_z1(CH - 1)
            make_z2(CH - 1)
            banks = [acc1[0], acc1[1], acc0, turn_x2_ps]
            for t in range(4):
                act.wait_ge(h1_summed, t + 1)
                nc.scalar.activation(h1[:, t], banks[t][:], ACT.Relu, bias=bias_top[:, t:t + 1]).then_inc(h1_made, 1)
            for t in range(2):
                act.wait_ge(h2_summed, t + 1)
                nc.scalar.activation(h2[:, t], g_ps[t][:], ACT.Relu, bias=bias_top[:, 4 + t:5 + t]).then_inc(h2_made, 1)
            act.wait_ge(y_summed, 1)
            nc.scalar.activation(y_sb[:], turn_x0[0:1, :], ACT.Copy).then_inc(y_made, 1)


def kernel(**inputs):
    import numpy as _np
    import concourse.bacc as _bacc
    from concourse import mybir as _mybir
    from concourse.bass_utils import run_bass_kernel_spmd as _run

    nc = _bacc.Bacc("TRN2", target_bir_lowering=False, num_devices=1)
    arrays = {}

    def take(name, a):
        a = _np.ascontiguousarray(a)
        arrays[f"in_{name}"] = a
        return nc.dram_tensor(f"in_{name}", a.shape, _mybir.dt.from_np(a.dtype), kind="ExternalInput").ap()

    ap = {name: take(name, a) for name, a in inputs.items()}
    ident = take("ident", _np.eye(128, dtype=_np.float32))
    mask = take("mask", _np.repeat(_np.eye(8, dtype=_np.float32), 16, axis=0))
    out = nc.dram_tensor("out", (512, 1), _mybir.dt.float32, kind="ExternalOutput").ap()
    build(nc, ap["dense_ctx"], ap["ids"], [ap[f"tbl_{f}"] for f in range(39)], ap["W_top1"], ap["b_top1"],
          ap["W_top2"], ap["b_top2"], ap["W_top3"], ap["L0_rec_W0"], ap["L0_rec_b0"], ap["L0_rec_W1"],
          ap["L0_rec_b1"], ap["L0_rec_W2"], ap["L0_rec_b2"], ident, mask, out)
    r = _run(nc, [arrays], core_ids=[0])
    return r.results[0]["out"]
```

```python
from contextlib import ExitStack

import concourse.bass as bass
from concourse import mybir

F32 = mybir.dt.float32
F32R = mybir.dt.float32r
I32 = mybir.dt.int32
U32 = mybir.dt.uint32
ALU = mybir.AluOpType
ACT = mybir.ActivationFunctionType
AX = mybir.AxisListType

P = 128
B, NF, D, H = 512, 39, 16, 128
CH = B // P
SPC = 4
STEPS = CH * SPC
N = B * D // STEPS
BS = N // D
JL, KL = 8, 16
NJ = 5
NK0 = 3
NK1 = H // KL
ROWS_X0 = NK0 * KL
JLAST = NF - (NJ - 1) * JL
GB = P // D
GRP = N // P
NG = NF + 1

L0_TILES = [(0, 0, 0), (1, 0, 0), (0, 1, 1), (1, 1, 1), (2, 1, 0), (3, 1, 0), (4, 0, 1), (4, 1, 1), (4, 2, 0)]
L0_UNITS = [(0, 2), (2, 2), (4, 2), (6, 2), (8, 1)]

A_UNITS = [(J, K) for K in (0, 2) for J in range(NJ)]
B_UNITS = [(J, K) for K in (4, 6) for J in range(NJ)]

UNITS = ([("A", u) for u in A_UNITS] + [("B", u) for u in B_UNITS])
L0_FIRST = 7
for n_, u_ in enumerate(L0_UNITS):
    UNITS.insert(L0_FIRST + 2 * n_, ("L0", u_))
NU = len(UNITS)
L0_ALL = [i for i, (kind, _) in enumerate(UNITS) if kind == "L0"]
L0_LAST = L0_ALL[-1]
A_LAST = max(i for i, (kind, _) in enumerate(UNITS) if kind == "A")
B_FIRST = min(i for i, (kind, _) in enumerate(UNITS) if kind == "B")
SPLIT = [i for i in range(0, NU - 1, 2) if i not in L0_ALL]


def is_split(i):
    return i in SPLIT


SPLIT_PER_STEP = len(SPLIT)
WHOLE_PER_STEP = NU - SPLIT_PER_STEP
RING_W = 4
RING_S = 3
assert SPC * SPLIT_PER_STEP % RING_S == 0 and SPC * WHOLE_PER_STEP % RING_W == 0


class Step:

    def __init__(self, c, q, has_next=True):
        self.c, self.q, self.has_next = c, q, has_next
        self.static = isinstance(c, int)

    def count(self, per_step, const):
        return self.c * (SPC * per_step) + (per_step * self.q + const)

    def units(self):
        if self.q == -1:
            return L0_ALL
        rest = [i for i in range(NU) if i not in L0_ALL]
        if not self.has_next:
            return rest
        if self.static and self.c * SPC + self.q == 0:
            return L0_ALL + rest
        return list(range(NU))

    def place(self, i, split, through=0):
        order = self.units()
        upto = order if i is None else order[:order.index(i) + through]
        before = sum(is_split(u) == split for u in upto)
        if self.q == -1:
            return before, before
        per = SPLIT_PER_STEP if split else WHOLE_PER_STEP
        const = before + sum(is_split(u) == split for u in L0_ALL)
        return self.count(per, const), per * self.q + const

    def done(self, i, split):
        return self.place(i, split, 1)[0]


def wait(eng, sem, value):
    if isinstance(value, int) and value <= 0:
        return
    eng.wait_ge(sem, value)


def build(nc, dense_ctx, ids, tables, w_top1, b_top1, w_top2, b_top2, w_top3, w0, b0, w1, b1, w2, b2,
          ident_in, mask_in, out):
    ctx = ExitStack()
    with ctx:
        def sb(name, shape, dt=F32):
            return ctx.enter_context(nc.sbuf_tensor(name, shape, dt))

        def ps(name):
            return ctx.enter_context(nc.psum_tensor(name, [P, 512], F32))

        def sem(name):
            return ctx.enter_context(nc.semaphore(name))

        x0_dram = nc.dram_tensor("x0_scratch", [ROWS_X0, B * D], F32).ap()
        x1_dram = nc.dram_tensor("x1_scratch", [STEPS, H, N], F32).ap()

        l1_split, l1_whole = ([(u[0], u[1] + m) for i, (kind, u) in enumerate(UNITS) if kind != "L0"
                               and is_split(i) == split for m in range(2)] for split in (True, False))
        l1_split.sort(key=lambda t: t[0] == NJ - 1)
        l1_whole.sort(key=lambda t: t[0] == NJ - 1)
        w1_head = sb("w1_head", [P, len(l1_split), H], F32R)
        w1_tail = sb("w1_tail", [P, len(l1_split), H], F32R)
        w1_whole = sb("w1_whole", [P, len(l1_whole), H])
        w0_tiles = sb("w0_tiles", [P, len(L0_TILES), H])
        w2_tiles = sb("w2_tiles", [P, NF, H])
        ident = sb("ident", [P, P])
        mask = sb("mask", [P, GB])
        bias = sb("bias", [P, 3])
        bias16 = sb("bias16", [P, 1])
        bias_top = sb("bias_top", [P, 6])
        wt3 = sb("wt3", [P, 2])
        dense = sb("dense", [P, CH, 16])
        dense_t = sb("dense_t", [16, B])

        g_sum = sb("g_sum", [P, NG, P])
        raw = g_sum[:, 0:NF, :].rearrange("p a b -> p (a b)")

        rep_j = sb("rep_j", [P, 2, NJ, N])
        rep_k = sb("rep_k", [P, NK0, N])
        rep_x1 = sb("rep_x1", [P, NK1, N])
        z_whole = sb("z_whole", [P, RING_W, 2, N])
        z_bytes = z_whole[:].rearrange("p r t n -> p (r t n)")
        w0_raw = z_bytes[:, 0:NF * NF]
        w0_sym = z_bytes[:, 2048:2048 + len(L0_TILES) * P].rearrange(
            "p (t j k) -> p t j k", t=len(L0_TILES), j=JL)
        z_full = sb("z_full", [P, RING_S, 2, N])
        z_head = sb("z_head", [P, RING_S, 2, N], F32R)
        z_tail = sb("z_tail", [P, RING_S, 2, N], F32R)

        idx = sb("idx", [P, NF], I32)
        emb = sb("emb", [P, NF, D])
        x0_sb = sb("x0_sb", [P, P * D])
        x0_p = sb("x0_p", [P, CH * GRP, NF])
        x0_blk = sb("x0_blk", [P, GRP, NG, GB])
        x1_sb = sb("x1_sb", [P, N])
        x2_sb = sb("x2_sb", [P, N])
        x2_p = sb("x2_p", [P, GRP, H])
        z0 = sb("z0", [P, B])
        z1 = sb("z1", [P, B])
        z2 = sb("z2", [P, B])
        wt1 = rep_j[:, 0, 0:4, :]
        wt2 = rep_k[:].rearrange("p a n -> p (a n)")[:, 0:4 * 256].rearrange("p (t m) -> p t m", t=4)
        h1 = rep_x1[:, 0:4, :]
        h2 = rep_x1[:, 4:6, :]
        y_sb = sb("y_sb", [1, B])

        acc1 = [ps("acc1_even"), ps("acc1_odd")]
        acc0 = ps("acc0")
        turn_x2_ps = ps("turn_x2")
        turn_x0 = ps("turn_x0")
        g_ps = [ps("g_even"), ps("g_odd")]
        z2_ps = ps("z2_ps")
        h1_ps = [acc1[0], acc0, turn_x0, acc1[1]]

        ld_const, ld_w0, ld_w1, ld_w2, ld_top = sem("ld_const"), sem("ld_w0"), sem("ld_w1"), sem("ld_w2"), sem("ld_top")
        ld_dense = sem("ld_dense")
        ld_idx, gathered = sem("ld_idx"), sem("gathered")
        x0_stored, x1_stored = sem("x0_stored"), sem("x1_stored")
        ld_rep_j = [sem("ld_rep_j_even"), sem("ld_rep_j_odd")]
        ld_rep_k, ld_x1_a, ld_x1_b = sem("ld_rep_k"), sem("ld_x1_a"), sem("ld_x1_b")
        out_stored = sem("out_stored")
        sp_passed, pe_passed, pool_passed = sem("sp_passed"), sem("pe_passed"), sem("pool_passed")
        w0_staged, w0_zeroed, w_turned, w_copied, w_tailed = (sem("w0_staged"), sem("w0_zeroed"), sem("w_turned"),
                                                              sem("w_copied"), sem("w_tailed"))
        b2_scaled = sem("b2_scaled")
        whole_ready, whole_used = sem("whole_ready"), sem("whole_used")
        full_ready, head_ready, tail_ready, split_used = (sem("full_ready"), sem("head_ready"), sem("tail_ready"),
                                                          sem("split_used"))
        x1_made, x2_made, z0_made = sem("x1_made"), sem("x2_made"), sem("z0_made")
        emb_turned, x0_made, x0_zeroed, x0_turned, x0p_made = (sem("emb_turned"), sem("x0_made"), sem("x0_zeroed"),
                                                               sem("x0_turned"), sem("x0p_made"))
        blk_ones, blk_made, x2_turned, x2p_made = sem("blk_ones"), sem("blk_made"), sem("x2_turned"), sem("x2p_made")
        g_summed, g_made, z1_made, z2_summed, z2_made = (sem("g_summed"), sem("g_made"), sem("z1_made"),
                                                         sem("z2_summed"), sem("z2_made"))
        dense_turned, dense_made = sem("dense_turned"), sem("dense_made")
        h1_summed, h1_made, h2_summed, h2_made, y_summed, y_made = (
            sem("h1_summed"), sem("h1_made"), sem("h2_summed"), sem("h2_made"), sem("y_summed"), sem("y_made"))

        w1_view = raw.rearrange("h (j k) -> h j k", j=NF).rearrange("h j (l g) -> h j l g", g=NK1)
        turns = []

        def w1_source(J, K):
            return w1_view[:, J * JL:min(J * JL + JL, NF), :, K]

        for a in range(0, len(L0_TILES), 4):
            ts = list(range(a, min(a + 4, len(L0_TILES))))
            turns.append(([w0_sym[:, t].rearrange("p j k -> p (j k)") for t in ts], P, "w0", a))
        for kind, tiles in (("split", l1_split), ("whole", l1_whole)):
            a = 0
            while a < len(tiles):
                rows = JLAST * KL if tiles[a][0] == NJ - 1 else P
                b_ = a
                while b_ < len(tiles) and b_ - a < 4 and (tiles[b_][0] == NJ - 1) == (rows < P):
                    b_ += 1
                turns.append(([w1_source(*t) for t in tiles[a:b_]], rows, kind, a))
                a = b_
        last_w1_turn = len(turns)
        for a in range(0, NF, 4):
            js = list(range(a, min(a + 4, NF)))
            turns.append(([raw[:, j * H:(j + 1) * H] for j in js], P, "w2", a))
        turn_bank = [turn_x2_ps, g_ps[0], g_ps[1], z2_ps]
        splits_upto = [sum(t[2] == "split" for t in turns[:g + 1]) for g in range(len(turns))]

        def turn_dst(kind, rows, a, n):
            dst = {"w0": w0_tiles, "split": w1_head, "whole": w1_whole, "w2": w2_tiles}[kind]
            return dst[0:rows, a:a + n, :]

        PE_TURN_X2, PE_G = 5, (9, 16)
        PE_EMB = (3, 8, 13, 18)
        PE_X0P = (9, 13, 17, 21)
        PE_Z2 = 21
        TAIL_LAG = 2
        DVE_LAG = 5
        LAG = 2

        def used(eng, st, i):
            wait(eng, split_used if is_split(i) else whole_used, st.done(i, is_split(i)))

        def k_rows(J):
            return JLAST * KL if J == NJ - 1 else P

        block = ctx.enter_context(nc.Block())

        @block.sync
        def _(sp):
            def settle():
                sp.sem_inc(sp_passed, 1)

            sp.dma_start(ident[:], ident_in).then_inc(ld_const, 16)
            sp.dma_start(mask[:], mask_in).then_inc(ld_const, 16)
            for i, b_ in enumerate((b0, b1, b2)):
                sp.dma_start(bias[:, i:i + 1], b_.rearrange("(p o) -> p o", o=1)).then_inc(ld_const, 16)
            sp.dma_start(w0_raw, w0).then_inc(ld_w0, 16)
            sp.dma_start(raw, w1).then_inc(ld_w1, 16)

            def store_x0(c):
                sp.wait_ge(x0_made, c * 4 + 4)
                settle()
                sp.dma_start(x0_dram[:, bass.ds(c * (P * D), P * D)], x0_sb[0:ROWS_X0, :]).then_inc(x0_stored, 16)

            def load_rep_j(st):
                settle()
                cols = bass.ds(st.count(N, 0), N)
                for J in range(NJ):
                    src = x0_dram[J * JL:(J + 1) * JL, cols].unsqueeze(1).to_broadcast([JL, KL, N])
                    sp.dma_start(rep_j[:, st.q % 2, J], src).then_inc(ld_rep_j[st.q % 2], 16)

            def load_rep_k(st):
                settle()
                cols = bass.ds(st.count(N, 0), N)
                for K in range(NK0):
                    src = x0_dram[K * KL:(K + 1) * KL, cols].unsqueeze(0).to_broadcast([JL, KL, N])
                    sp.dma_start(rep_k[:, K], src).then_inc(ld_rep_k, 16)

            def mults_done(st, i):
                settle()
                wait(sp, whole_ready, st.done(i, False))
                settle()
                wait(sp, full_ready, st.done(i, True))
                settle()

            def load_x1(st, half, semaphore):
                settle()
                src = x1_dram[bass.ds(st.count(1, 0), 1)].rearrange("s (l g) n -> (s l) g n", g=NK1)
                src = src[:, half * 4:half * 4 + 4, :].rearrange("l g n -> l (g n)").unsqueeze(0).to_broadcast([JL, KL, 4 * N])
                sp.dma_start(rep_x1[:, half * 4:half * 4 + 4, :], src).then_inc(semaphore, 16)

            def store_x1(st):
                wait(sp, x1_made, st.count(1, 1))
                settle()
                dst = x1_dram[bass.ds(st.count(1, 0), 1)].rearrange("s k n -> (s k) n")
                sp.dma_start(dst, x1_sb[:]).then_inc(x1_stored, 16)
                wait(sp, x1_stored, st.count(16, 16))
                settle()

            for t in range(2):
                sp.dma_start(wt3[:, t:t + 1], w_top3[t * P:(t + 1) * P]).then_inc(ld_dense, 16)
            for t in range(6):
                b_ = b_top1[t * P:(t + 1) * P] if t < 4 else b_top2[(t - 4) * P:(t - 3) * P]
                sp.dma_start(bias_top[:, t:t + 1], b_.rearrange("(p o) -> p o", o=1)).then_inc(ld_dense, 16)
            sp.dma_start(dense[:], dense_ctx.rearrange("(c p) f -> p c f", p=P)).then_inc(ld_dense, 16)
            sp.wait_ge(w_turned, last_w1_turn)
            sp.dma_start(raw, w2).then_inc(ld_w2, 16)

            store_x0(0)
            sp.wait_ge(x0_stored, 16)
            load_rep_j(Step(0, 0))
            load_rep_k(Step(0, 0))
            load_rep_j(Step(0, 1))
            mults_done(Step(0, -1), None)
            load_rep_k(Step(0, 1))
            store_x1(Step(0, 0))
            load_x1(Step(0, 0), 0, ld_x1_a)
            load_x1(Step(0, 0), 1, ld_x1_b)
            store_x1(Step(0, 1))
            mults_done(Step(0, 0), A_LAST)
            load_x1(Step(0, 1), 0, ld_x1_a)

            def step(c, q, has_next=True, chunk_after=False):
                st, prev, nxt = Step(c, q, has_next), Step(c, q - 1), Step(c, q + 1)
                mults_done(prev, None)
                load_x1(st, 1, ld_x1_b)
                if not has_next:
                    sp.dma_start(wt1[:, 0:3, :], w_top1[0:3 * P].rearrange("(t p) m -> p t m", p=P)).then_inc(ld_top, 16)
                    sp.dma_start(wt1[0:16, 3, :], w_top1[3 * P:3 * P + 16]).then_inc(ld_top, 16)
                    sp.dma_start(wt2, w_top2.rearrange("(t p) m -> p t m", p=P)).then_inc(ld_top, 16)
                    return
                if q == 3 and chunk_after:
                    wait(sp, x0_stored, c * 16 + 32)
                load_rep_j(nxt)
                load_rep_k(nxt)
                store_x1(nxt)
                mults_done(st, A_LAST)
                load_x1(nxt, 0, ld_x1_a)
                if q == 2 and chunk_after:
                    store_x0(c + 1)

            step(0, 1)
            with sp.Fori(0, CH - 1) as c:
                for q in range(2, 6):
                    step(c, q, chunk_after=True)
            for q in range(2, 4):
                step(CH - 1, q, has_next=q < 3)
            sp.wait_ge(y_made, 1)
            sp.dma_start(out.rearrange("b o -> o b"), y_sb[:]).then_inc(out_stored, 16)
            sp.wait_ge(out_stored, 16)

        @block.gpsimd
        def _(pool):
            nc.gpsimd.memset(x0_sb[:], 0.0).then_inc(x0_zeroed, 1)

            def gather(c):
                if not (isinstance(c, int) and c == 0):
                    pool.wait_ge(gathered, c * (16 * NF))
                pool.dma_start(idx[:], ids[bass.ds(c * P, P), :]).then_inc(ld_idx, 16)
                pool.wait_ge(ld_idx, c * 16 + 16)
                if not (isinstance(c, int) and c == 0):
                    pool.wait_ge(emb_turned, c * 4)
                pool.sem_inc(pool_passed, 1)
                for f in range(NF):
                    pool.indirect_dma_start(
                        out=emb[:, f, :], out_offset=None, in_=tables[f],
                        in_offset=bass.IndirectOffsetOnAxis(ap=idx[:, f:f + 1].bitcast(U32), axis=0)
                    ).then_inc(gathered, 16)

            gather(0)
            with pool.Fori(1, CH) as c:
                gather(c)

        @block.tensor
        def _(pe):
            turned = [0]

            def turn_weights(g):
                srcs, rows, kind, _ = turns[g]
                if g >= len(turn_bank):
                    old = g - len(turn_bank)
                    pe.wait_ge(w_copied, old + 1)
                    wait(pe, w_tailed, splits_upto[old])
                for m, src in enumerate(srcs):
                    mm = pe.transpose(turn_bank[g % len(turn_bank)][0:rows, m * P:(m + 1) * P], src, ident[:])
                mm.then_inc(w_turned, 1)

            def turn_emb(c, part):
                if part == 0:
                    pe.wait_ge(gathered, c * (16 * NF) + 16 * NF)
                    wait(pe, x0p_made, c * 4)
                wait(pe, x0_made, c * 4 + part)
                pe.sem_inc(pe_passed, 1)
                for m in range(4):
                    mm = pe.transpose(turn_x0[0:NF, m * P:(m + 1) * P], emb[:, :, 4 * part + m], ident[:])
                mm.then_inc(emb_turned, 1)

            def turn_x0p(c, part):
                if part == 0:
                    pe.wait_ge(x0_made, c * 4 + 4)
                wait(pe, x0p_made, c * 4 + part)
                for m in range(GRP):
                    g = part * GRP + m
                    mm = pe.transpose(turn_x0[:, m * P:(m + 1) * P], x0_sb[:, g * P:(g + 1) * P], ident[:])
                mm.then_inc(x0_turned, 1)

            def unit(st, i):
                kind, u = UNITS[i]
                split = is_split(i)
                count, at = st.place(i, split)
                slot = at % (RING_S if split else RING_W)
                wait(pe, tail_ready if split else whole_ready, count + 1)
                if kind == "L0":
                    tiles = [(w0_tiles[:, t], P, t == 0, t == len(L0_TILES) - 1) for t in range(u[0], u[0] + u[1])]
                    acc = acc0
                    if i == L0_FIRST:
                        wait(pe, x1_made, st.count(1, 1))
                else:
                    J, K = u
                    tiles = []
                    for m in range(2):
                        r, first = k_rows(J), i == 0 and m == 0
                        last = i == NU - 1 and m == 1
                        if split:
                            n = l1_split.index((J, K + m))
                            tiles.append(((w1_head[0:r, n], w1_tail[0:r, n]), r, first, last))
                        else:
                            tiles.append((w1_whole[0:r, l1_whole.index((J, K + m))], r, first, last))
                    acc = acc1[st.q % 2]
                    if i == 0:
                        wait(pe, x2_made, st.count(1, -1))
                for m, (w, r, first, last) in enumerate(tiles):
                    if split:
                        head, tail = z_head[0:r, slot, m], z_tail[0:r, slot, m]
                        pe.matmul(acc[:], w[0], head, start=first, stop=False)
                        pe.matmul(acc[:], w[0], tail, start=False, stop=False)
                        mm = pe.matmul(acc[:], w[1], head, start=False, stop=last)
                    else:
                        mm = pe.matmul(acc[:], w, z_whole[0:r, slot, m], start=first, stop=last)
                mm.then_inc(split_used if split else whole_used, 1)

            def turn_x2(st):
                wait(pe, x2_made, st.count(1, 1))
                wait(pe, x2p_made, st.count(1, 0))
                for g in range(GRP):
                    mm = pe.transpose(turn_x2_ps[:, g * P:(g + 1) * P], x2_sb[:, g * P:(g + 1) * P], ident[:])
                mm.then_inc(x2_turned, 1)

            def g_products(st, groups):
                if groups[0] == 0:
                    wait(pe, x2p_made, st.count(1, 1))
                    wait(pe, blk_made, st.count(1, 1))
                for g in groups:
                    if g >= 2:
                        pe.wait_ge(g_made, st.count(GRP, g - 1))
                    pe.matmul(g_ps[g % 2][:, 0:NG * GB], x2_p[:, g], x0_blk[:, g].rearrange("p j b -> p (j b)"),
                              start=True, stop=True).then_inc(g_summed, 1)

            def l2_product(c):
                wait(pe, g_made, c * (GRP * SPC) + GRP * SPC)
                for j in range(NF):
                    mm = pe.matmul(z2_ps[:, 0:P], w2_tiles[:, j], g_sum[:, j, :], start=j == 0, stop=j == NF - 1)
                mm.then_inc(z2_summed, 1)

            def step(c, q, has_next=True, chunk_next=None):
                st, prev = Step(c, q, has_next), Step(c, q - 1)
                for n, i in enumerate(st.units()):
                    if not (st.static and c * SPC + q == 0):
                        if n == PE_TURN_X2:
                            turn_x2(prev)
                        if n in PE_G:
                            g_products(prev, (0, 1) if n == PE_G[0] else (2, 3))
                    if q == 2 and chunk_next is not None and n in PE_EMB:
                        turn_emb(chunk_next, PE_EMB.index(n))
                    if q == 4 and n in PE_X0P:
                        turn_x0p(chunk_next, PE_X0P.index(n))
                    if q == 4 and n == PE_Z2:
                        l2_product(c)
                    unit(st, i)

            pe.wait_ge(ld_const, 16 * 5)
            pe.wait_ge(w0_staged, len(L0_TILES))
            for g in range(last_w1_turn):
                if turns[g][2] != "w0":
                    pe.wait_ge(ld_w1, 16)
                turn_weights(g)
            pe.wait_ge(ld_w2, 16)
            for g in range(last_w1_turn, len(turns)):
                turn_weights(g)
            pe.wait_ge(ld_dense, 16 * 9)
            pe.wait_ge(w_copied, len(turns))
            wait(pe, w_tailed, splits_upto[-1])
            for m in range(CH):
                mm = pe.transpose(z2_ps[0:16, m * P:(m + 1) * P], dense[:, m], ident[:])
            mm.then_inc(dense_turned, 1)
            for part in range(4):
                turn_emb(0, part)
            first = Step(0, -1)
            for i in first.units():
                unit(first, i)
            for part in range(SPC):
                turn_x0p(0, part)
            step(0, 0)
            step(0, 1)
            with pe.Fori(0, CH - 1) as c:
                for q in range(2, 6):
                    step(c, q, chunk_next=c + 1)
            for q in range(2, 4):
                step(CH - 1, q, has_next=q < 3)

            last = Step(CH - 1, 3, False)

            def top1(m, t, **flags):
                rhs = (z0[:], z1[:], z2[:], dense_t[:])[t]
                w = wt1[0:16, 3, m * P:(m + 1) * P] if t == 3 else wt1[:, t, m * P:(m + 1) * P]
                return pe.matmul(h1_ps[m][:], w, rhs, **{"start": False, "stop": False, **flags})

            pe.wait_ge(ld_top, 16 * 3)
            pe.wait_ge(z0_made, STEPS)
            pe.wait_ge(dense_made, 1)
            top1(0, 3, start=True)
            top1(0, 0)
            turn_x2(last)
            top1(1, 3, start=True)
            top1(1, 0)
            g_products(last, (0, 1))
            top1(2, 3, start=True)
            top1(2, 0)
            g_products(last, (2, 3))
            top1(3, 3, start=True)
            top1(3, 0)
            pe.wait_ge(z1_made, CH)
            for m in range(4):
                top1(m, 1)
            l2_product(CH - 1)
            pe.wait_ge(z2_made, CH)
            for m in range(4):
                top1(m, 2, stop=True).then_inc(h1_summed, 1)
            for t in range(4):
                pe.wait_ge(h1_made, t + 1)
                for m in range(2):
                    mm = pe.matmul(g_ps[m][:], wt2[:, t, m * P:(m + 1) * P], h1[:, t], start=t == 0, stop=t == 3)
                    if t == 3:
                        mm.then_inc(h2_summed, 1)
            for t in range(2):
                pe.wait_ge(h2_made, t + 1)
                mm = pe.matmul(turn_x2_ps[0:1, :], wt3[:, t:t + 1], h2[:, t], start=t == 0, stop=t == 1)
            mm.then_inc(y_summed, 1)

        @block.vector
        def _(dve):
            nc.vector.memset(w0_sym, 0.0).then_inc(w0_zeroed, 1)
            dve.wait_ge(w0_zeroed, 1)
            dve.wait_ge(ld_w0, 16)
            w0_jk = w0_raw.rearrange("h (j k) -> h j k", j=NF)
            for t, (J, K, both) in enumerate(L0_TILES):
                js, ks = slice(J * JL, min(J * JL + JL, NF)), slice(K * KL, min(K * KL + KL, NF))
                dst = w0_sym[:, t, 0:js.stop - js.start, 0:ks.stop - ks.start]
                if both:
                    ins = nc.vector.tensor_tensor(dst, w0_jk[:, js, ks], w0_jk[:, ks, js].rearrange("h k j -> h j k"),
                                                  ALU.add)
                else:
                    ins = nc.vector.tensor_copy(dst, w0_jk[:, js, ks])
                ins.then_inc(w0_staged, 1)
            dve.wait_ge(ld_const, 16 * 5)
            nc.vector.tensor_scalar(bias16[:], bias[:, 2:3], float(D), None, ALU.mult).then_inc(b2_scaled, 1)
            for g in range(GRP):
                nc.vector.tensor_copy(x0_blk[:, g, NF, :], mask[:]).then_inc(blk_ones, 1)
            n = 0
            for g, (srcs, rows, kind, a) in enumerate(turns):
                if kind == "split":
                    dve.wait_ge(w_copied, g + 1)
                    m = len(srcs)
                    nc.vector.tensor_tensor(
                        w1_tail[0:rows, a:a + m], turn_bank[g % len(turn_bank)][0:rows, 0:m * P].rearrange(
                            "p (t h) -> p t h", t=m),
                        w1_head[0:rows, a:a + m].bitcast(F32), ALU.subtract).then_inc(w_tailed, 1)

            def operands(st, i):
                kind, u = UNITS[i]
                if kind == "L0":
                    slot = (st.q + 1) % 2
                    tiles = L0_TILES[u[0]:u[0] + u[1]]
                    J, K = tiles[0][0], tiles[0][1]
                    if len(tiles) == 1:
                        return rep_j[:, slot, J:J + 1], rep_k[:, K:K + 1]
                    if tiles[1][0] > J:
                        return rep_j[:, slot, J:J + 2], rep_k[:, K:K + 1].to_broadcast([P, 2, N])
                    return rep_j[:, slot, J:J + 1].to_broadcast([P, 2, N]), rep_k[:, K:K + 2]
                J, K = u
                return rep_j[:, st.q % 2, J:J + 1].to_broadcast([P, 2, N]), rep_x1[:, K:K + 2]

            def tail(st, i):
                count, at = st.place(i, True)
                slot = at % RING_S
                dve.wait_ge(head_ready, count + 1)
                wait(dve, split_used, count + (1 - RING_S))
                nc.vector.tensor_tensor(z_tail[:, slot], z_full[:, slot],
                                        z_head[:, slot].bitcast(F32), ALU.subtract).then_inc(tail_ready, 1)

            def product(st, i):
                split = is_split(i)
                count, at = st.place(i, split)
                slot = at % (RING_S if split else RING_W)
                if i == L0_FIRST:
                    nq = st.q + 1
                    dve.wait_ge(ld_rep_j[nq % 2], st.c * (16 * NJ * SPC // 2) + 16 * NJ * (nq // 2 + 1))
                    dve.wait_ge(ld_rep_k, st.count(16 * NK0, 32 * NK0))
                if i == 0:
                    dve.wait_ge(ld_x1_a, st.count(16, 16))
                if i == B_FIRST:
                    dve.wait_ge(ld_x1_b, st.count(16, 16))
                in0, in1 = operands(st, i)
                tiles = in0.shape[1]
                if split:
                    wait(dve, tail_ready, count + (1 - RING_S))
                    nc.vector.tensor_tensor(z_full[:, slot], in0, in1, ALU.mult).then_inc(full_ready, 1)
                else:
                    wait(dve, whole_used, count + (1 - RING_W))
                    nc.vector.tensor_tensor(z_whole[:, slot, 0:tiles], in0, in1, ALU.mult).then_inc(whole_ready, 1)

            def sum_x1(st):
                dve.wait_ge(x1_made, st.count(1, 1))
                nc.vector.tensor_reduce(z0[:, bass.ds(st.count(BS, 0), BS)], x1_sb[:].rearrange("p (b d) -> p b d", d=D),
                                        AX.X, ALU.add).then_inc(z0_made, 1)

            def step(c, q, has_next=True):
                st = Step(c, q, has_next)
                late = []
                order = st.units()
                for n, i in enumerate(order):
                    product(st, i)
                    if late and (order.index(late[0]) <= n - TAIL_LAG):
                        tail(st, late.pop(0))
                    if is_split(i):
                        late.append(i)
                    if st.static and c * SPC + q == 0 and n == order.index(L0_LAST):
                        sum_x1(st)
                    if has_next and q >= 0 and n == order.index(L0_LAST) + DVE_LAG:
                        sum_x1(Step(c, q + 1))

                assert not late

            dve.wait_ge(w_turned, sum(t[2] == "w0" for t in turns))
            step(0, -1)
            step(0, 0)
            step(0, 1)
            with dve.Fori(0, CH - 1) as c:
                for q in range(2, 6):
                    step(c, q)
            for q in range(2, 4):
                step(CH - 1, q, has_next=q < 3)

        @block.scalar
        def _(act):
            act.wait_ge(ld_const, 16 * 5)

            def copy_turned(g):
                srcs, rows, kind, a = turns[g]
                act.wait_ge(w_turned, g + 1)
                m = len(srcs)
                nc.scalar.activation(turn_dst(kind, rows, a, m),
                                     turn_bank[g % len(turn_bank)][0:rows, 0:m * P].rearrange("p (t h) -> p t h", t=m),
                                     ACT.Copy).then_inc(w_copied, 1)

            def copy_emb(c, part):
                if part == 0:
                    wait(act, x0_stored, c * 16)
                    wait(act, x0_turned, c * SPC)
                act.wait_ge(emb_turned, c * 4 + (part + 1))
                dst = x0_sb[0:NF, :].rearrange("j (b d) -> j b d", d=D)[:, :, 4 * part:4 * part + 4]
                nc.scalar.activation(dst.rearrange("j b m -> j m b"),
                                     turn_x0[0:NF, :].rearrange("j (m b) -> j m b", m=4), ACT.Copy).then_inc(x0_made, 1)

            def copy_x0p(c, part):
                act.wait_ge(x0_turned, c * SPC + (part + 1))
                nc.scalar.activation(x0_p[:, part * GRP:(part + 1) * GRP, :],
                                     turn_x0[:].rearrange("p (g j) -> p g j", g=GRP)[:, :, 0:NF],
                                     ACT.Copy).then_inc(x0p_made, 1)

            def make_x1(st):
                used(act, Step(st.c, st.q - 1), L0_LAST)
                wait(act, x1_stored, st.count(16, 0))
                wait(act, z0_made, st.count(1, 0))
                nc.scalar.activation(x1_sb[:], acc0[:], ACT.Identity, bias=bias[:, 0:1]).then_inc(x1_made, 1)

            def make_x2(st):
                used(act, st, NU - 1)
                wait(act, x2_turned, st.count(1, 0))
                nc.scalar.activation(x2_sb[:], acc1[st.q % 2][:], ACT.Identity, bias=bias[:, 1:2]).then_inc(x2_made, 1)

            def make_blk(st):
                wait(act, g_summed, st.count(GRP, 0))
                part = st.q % SPC
                act.wait_ge(x0p_made, st.count(1, SPC - part))
                for b_ in range(GB):
                    ins = nc.scalar.activation(x0_blk[:, :, 0:NF, b_], x0_p[:, part * GRP:(part + 1) * GRP, :], ACT.Copy,
                                               scale=mask[:, b_:b_ + 1])
                ins.then_inc(blk_made, 1)

            def make_x2p(st):
                act.wait_ge(x2_turned, st.count(1, 1))
                wait(act, g_summed, st.count(GRP, 0))
                nc.scalar.activation(x2_p[:], turn_x2_ps[:].rearrange("p (g h) -> p g h", g=GRP),
                                     ACT.Copy).then_inc(x2p_made, 1)

            def copy_g(st, groups):
                if st.q % SPC == 0 and groups[0] == 0:
                    wait(act, z2_summed, st.c + st.q // SPC)
                for g in groups:
                    act.wait_ge(g_summed, st.count(GRP, g + 1))
                    b_ = (st.q % SPC) * BS + g * GB
                    nc.scalar.activation(g_sum[:, :, b_:b_ + GB],
                                         g_ps[g % 2][:, 0:NG * GB].rearrange("p (j b) -> p j b", b=GB),
                                         ACT.Copy).then_inc(g_made, 1)

            def make_z1(c):
                act.wait_ge(g_made, c * (SPC * GRP) + SPC * GRP)
                nc.scalar.activation(z1[:, bass.ds(c * P, P)], g_sum[:, NF, :], ACT.Copy).then_inc(z1_made, 1)

            def make_z2(c):
                act.wait_ge(z2_summed, c + 1)
                nc.scalar.activation(z2[:, bass.ds(c * P, P)], z2_ps[:, 0:P], ACT.Identity,
                                     bias=bias16[:]).then_inc(z2_made, 1)

            def head(st, i):
                count, at = st.place(i, True)
                slot = at % RING_S
                act.wait_ge(full_ready, count + 1)
                wait(act, split_used, count + (1 - RING_S))
                nc.scalar.activation(z_head[:, slot], z_full[:, slot], ACT.Copy).then_inc(head_ready, 1)

            def step(c, q, has_next=True, chunk_next=None):
                st, prev = Step(c, q, has_next), Step(c, q - 1)
                first = st.static and c * SPC + q == 0
                order = st.units()
                for n, i in enumerate(order):
                    if is_split(i):
                        head(st, i)
                    if not first:
                        if n == 2:
                            make_x2(prev)
                        if n == 3:
                            make_blk(prev)
                        if n == PE_TURN_X2 + LAG:
                            make_x2p(prev)
                        if n == PE_G[0] + LAG:
                            copy_g(prev, (0, 1))
                        if n == PE_G[1] + LAG:
                            copy_g(prev, (2, 3))
                    if q == 2 and chunk_next is not None and n - LAG in PE_EMB:
                        copy_emb(chunk_next, PE_EMB.index(n - LAG))
                    if q == 4 and n - LAG in PE_X0P:
                        copy_x0p(chunk_next, PE_X0P.index(n - LAG))
                    if has_next and n == order.index(L0_LAST) + LAG:
                        make_x1(Step(c, q + 1))
                    if q == 4 and n == PE_G[1] + LAG + 1:
                        make_z1(c)
                    if q == 4 and n == PE_Z2 + LAG:
                        make_z2(c)

            for g in range(len(turns)):
                copy_turned(g)
            act.wait_ge(dense_turned, 1)
            nc.scalar.activation(dense_t[:], z2_ps[0:16, :], ACT.Copy).then_inc(dense_made, 1)
            act.wait_ge(x0_zeroed, 1)
            for part in range(4):
                copy_emb(0, part)
            make_x1(Step(0, 0))
            for part in range(SPC):
                copy_x0p(0, part)
            act.wait_ge(blk_ones, GRP)
            act.wait_ge(b2_scaled, 1)
            step(0, 0)
            step(0, 1)
            with act.Fori(0, CH - 1) as c:
                for q in range(2, 6):
                    step(c, q, chunk_next=c + 1)
            for q in range(2, 4):
                step(CH - 1, q, has_next=q < 3)
            last = Step(CH - 1, 3, False)
            make_x2(last)
            make_blk(last)
            make_x2p(last)
            copy_g(last, (0, 1))
            copy_g(last, (2, 3))
            make_z1(CH - 1)
            make_z2(CH - 1)
            for t in range(4):
                act.wait_ge(h1_summed, t + 1)
                nc.scalar.activation(h1[:, t], h1_ps[t][:], ACT.Relu, bias=bias_top[:, t:t + 1]).then_inc(h1_made, 1)
            for t in range(2):
                act.wait_ge(h2_summed, t + 1)
                nc.scalar.activation(h2[:, t], g_ps[t][:], ACT.Relu, bias=bias_top[:, 4 + t:5 + t]).then_inc(h2_made, 1)
            act.wait_ge(y_summed, 1)
            nc.scalar.activation(y_sb[:], turn_x2_ps[0:1, :], ACT.Copy).then_inc(y_made, 1)


def kernel(**inputs):
    import numpy as _np
    import concourse.bacc as _bacc
    from concourse import mybir as _mybir
    from concourse.bass_utils import run_bass_kernel_spmd as _run

    nc = _bacc.Bacc("TRN2", target_bir_lowering=False, num_devices=1)
    arrays = {}

    def take(name, a):
        a = _np.ascontiguousarray(a)
        arrays[f"in_{name}"] = a
        return nc.dram_tensor(f"in_{name}", a.shape, _mybir.dt.from_np(a.dtype), kind="ExternalInput").ap()

    ap = {name: take(name, a) for name, a in inputs.items()}
    ident = take("ident", _np.eye(128, dtype=_np.float32))
    mask = take("mask", _np.repeat(_np.eye(8, dtype=_np.float32), 16, axis=0))
    out = nc.dram_tensor("out", (512, 1), _mybir.dt.float32, kind="ExternalOutput").ap()
    build(nc, ap["dense_ctx"], ap["ids"], [ap[f"tbl_{f}"] for f in range(39)], ap["W_top1"], ap["b_top1"],
          ap["W_top2"], ap["b_top2"], ap["W_top3"], ap["L0_rec_W0"], ap["L0_rec_b0"], ap["L0_rec_W1"],
          ap["L0_rec_b1"], ap["L0_rec_W2"], ap["L0_rec_b2"], ident, mask, out)
    r = _run(nc, [arrays], core_ids=[0])
    return r.results[0]["out"]
```

```python
from contextlib import ExitStack

import concourse.bass as bass
from concourse import mybir

F32 = mybir.dt.float32
F32R = mybir.dt.float32r
I32 = mybir.dt.int32
U32 = mybir.dt.uint32
ALU = mybir.AluOpType
ACT = mybir.ActivationFunctionType
AX = mybir.AxisListType

P = 128
B, NF, D, H = 512, 39, 16, 128
CH = B // P
SPC = 4
STEPS = CH * SPC
N = B * D // STEPS
BS = N // D
JL, KL = 8, 16
NJ = 5
ND = (NF + 1) // 2
DPT = P // NF
NT0 = -(-ND // DPT)
NK1 = H // KL
ROWS_X0 = NF + ND - 1
JLAST = NF - (NJ - 1) * JL
GB = P // D
GRP = N // P
NG = NF + 1

L0_UNITS = [(t, min(2, NT0 - t)) for t in range(0, NT0, 2)]


def l0_rows(t):
    return NF * min(DPT, ND - DPT * t)


A_UNITS = [(J, K) for K in (0, 2) for J in range(NJ)]
B_UNITS = [(J, K) for K in (4, 6) for J in range(NJ)]

UNITS = ([("A", u) for u in A_UNITS] + [("B", u) for u in B_UNITS])
L0_FIRST = 7
for n_, u_ in enumerate(L0_UNITS):
    UNITS.insert(L0_FIRST + 2 * n_, ("L0", u_))
NU = len(UNITS)
L0_ALL = [i for i, (kind, _) in enumerate(UNITS) if kind == "L0"]
L0_LAST = L0_ALL[-1]
A_LAST = max(i for i, (kind, _) in enumerate(UNITS) if kind == "A")
B_FIRST = min(i for i, (kind, _) in enumerate(UNITS) if kind == "B")
SPLIT_MORE = [i for i in range(0, NU, 2) if i not in L0_ALL] + [21]
SPLIT_LESS = [i for i in SPLIT_MORE if i not in (14, 21)]


def is_split(i, q):
    return i in (SPLIT_MORE if q % SPC < 2 else SPLIT_LESS)


def units_before(q, split):
    return sum(is_split(i, step) == split for step in range(q) for i in range(NU))


SPLIT_PER_CHUNK = units_before(SPC, True)
WHOLE_PER_CHUNK = units_before(SPC, False)
RING_W = 4
RING_F = 2
RING_S = 3
assert SPLIT_PER_CHUNK % RING_S == 0 and SPLIT_PER_CHUNK % RING_F == 0 and WHOLE_PER_CHUNK % RING_W == 0


class Step:

    def __init__(self, c, q, has_next=True):
        self.c, self.q, self.has_next = c, q, has_next
        self.static = isinstance(c, int)

    def count(self, per_step, const):
        return self.c * (SPC * per_step) + (per_step * self.q + const)

    def units(self):
        if self.q == -1:
            return L0_ALL
        rest = [i for i in range(NU) if i not in L0_ALL]
        if not self.has_next:
            return rest
        if self.static and self.c * SPC + self.q == 0:
            return L0_ALL + rest
        return list(range(NU))

    def place(self, i, split, through=0):
        order = self.units()
        upto = order if i is None else order[:order.index(i) + through]
        before = sum(is_split(u, self.q) == split for u in upto)
        if self.q == -1:
            return before, before
        per = SPLIT_PER_CHUNK if split else WHOLE_PER_CHUNK
        const = before + units_before(self.q, split) + sum(is_split(u, -1) == split for u in L0_ALL)
        return self.c * per + const, const

    def done(self, i, split):
        return self.place(i, split, 1)[0]


def wait(eng, sem, value):
    if isinstance(value, int) and value <= 0:
        return
    eng.wait_ge(sem, value)


def build(nc, dense_ctx, ids, tables, w_top1, b_top1, w_top2, b_top2, w_top3, w0, b0, w1, b1, w2, b2,
          ident_in, mask_in, out):
    ctx = ExitStack()
    with ctx:
        def sb(name, shape, dt=F32):
            return ctx.enter_context(nc.sbuf_tensor(name, shape, dt))

        def ps(name):
            return ctx.enter_context(nc.psum_tensor(name, [P, 512], F32))

        def sem(name):
            return ctx.enter_context(nc.semaphore(name))

        x0_dram = nc.dram_tensor("x0_scratch", [ROWS_X0, B * D], F32).ap()
        x1_dram = nc.dram_tensor("x1_scratch", [STEPS, H, N], F32).ap()

        l1_split, l1_whole = ([(u[0], u[1] + m) for i, (kind, u) in enumerate(UNITS) if kind != "L0"
                               and split in (is_split(i, 0), is_split(i, 2)) for m in range(2)]
                              for split in (True, False))
        l1_split.sort(key=lambda t: t[0] == NJ - 1)
        l1_whole.sort(key=lambda t: t[0] == NJ - 1)
        w1_head = sb("w1_head", [P, len(l1_split), H], F32R)
        w1_tail = sb("w1_tail", [P, len(l1_split), H], F32R)
        w1_whole = sb("w1_whole", [P, len(l1_whole), H])
        w0_tiles = sb("w0_tiles", [P, NT0, H])
        w2_tiles = sb("w2_tiles", [P, NF, H])
        ident = sb("ident", [P, P])
        mask = sb("mask", [P, GB])
        bias = sb("bias", [P, 3])
        bias16 = sb("bias16", [P, 1])
        bias_top = sb("bias_top", [P, 6])
        wt3 = sb("wt3", [P, 2])

        g_sum = sb("g_sum", [P, NG, P])
        raw = g_sum[:, 0:NF, :].rearrange("p a b -> p (a b)")

        rep_j = sb("rep_j", [P, 2, NJ, N])
        rep_l0 = sb("rep_l0", [P, 1 + NT0, N])
        rep_x1 = sb("rep_x1", [P, NK1, N])
        z_whole = sb("z_whole", [P, RING_W, 2, N])
        z_bytes = z_whole[:].rearrange("p r t n -> p (r t n)")
        w0_raw = z_bytes[:, 0:NF * NF]
        w0_sym = z_bytes[:, 2048:2048 + ND * NF].rearrange("p (d j) -> p d j", d=ND)
        z_full = sb("z_full", [P, RING_F, 2, N])
        z_head = sb("z_head", [P, RING_S, 2, N], F32R)
        z_tail = sb("z_tail", [P, RING_S, 2, N], F32R)

        idx = sb("idx", [P, NF], I32)
        emb = sb("emb", [P, NF, D])
        x0_sb = sb("x0_sb", [P, P * D])
        x0_p = sb("x0_p", [P, CH * GRP, NF])
        x0_blk = sb("x0_blk", [P, GRP, NG, GB])
        x1_sb = sb("x1_sb", [P, N])
        x2_sb = sb("x2_sb", [P, N])
        x2_p = sb("x2_p", [P, GRP, H])
        z0 = sb("z0", [P, B])
        z1 = sb("z1", [P, B])
        wt1 = rep_j[:, 0, 0:4, :]
        wt2 = rep_l0[:].rearrange("p a n -> p (a n)")[:, 0:4 * 256].rearrange("p (t m) -> p t m", t=4)
        dense = rep_l0[:, 2, 0:CH * 16].rearrange("p (c f) -> p c f", c=CH)
        dense_t = rep_l0[0:16, 3]
        h1 = rep_x1[:, 0:4, :]
        h2 = rep_x1[:, 4:6, :]
        z2 = rep_x1[:, 6, :]
        y_sb = x1_sb[0:1, :]

        acc1 = [ps("acc1_even"), ps("acc1_odd")]
        acc0 = ps("acc0")
        turn_x2_ps = ps("turn_x2")
        turn_x0 = ps("turn_x0")
        g_ps = [ps("g_even"), ps("g_odd")]
        z2_ps = ps("z2_ps")
        h1_ps = [acc1[0], acc0, turn_x0, acc1[1]]

        ld_const, ld_w0, ld_w1, ld_w2, ld_top = sem("ld_const"), sem("ld_w0"), sem("ld_w1"), sem("ld_w2"), sem("ld_top")
        ld_dense = sem("ld_dense")
        ld_idx, ld_idx_first, gathered = sem("ld_idx"), sem("ld_idx_first"), sem("gathered")
        x0_stored, x1_stored = sem("x0_stored"), sem("x1_stored")
        first_stored, ld_first, ld_second = sem("first_stored"), sem("ld_first"), sem("ld_second")
        ld_rep_j = [sem("ld_rep_j_even"), sem("ld_rep_j_odd")]
        ld_rep_l0, ld_x1_a, ld_x1_b = sem("ld_rep_l0"), sem("ld_x1_a"), sem("ld_x1_b")
        out_stored = sem("out_stored")
        sp_passed, pe_passed, pool_passed = sem("sp_passed"), sem("pe_passed"), sem("pool_passed")
        w0_staged, w_turned, w_copied, w_tailed = (sem("w0_staged"), sem("w_turned"),
                                                              sem("w_copied"), sem("w_tailed"))
        b2_scaled = sem("b2_scaled")
        whole_ready, whole_used = sem("whole_ready"), sem("whole_used")
        full_ready, head_ready, tail_ready, split_used = (sem("full_ready"), sem("head_ready"), sem("tail_ready"),
                                                          sem("split_used"))
        x1_made, x2_made, z0_made = sem("x1_made"), sem("x2_made"), sem("z0_made")
        emb_turned, x0_made, x0_zeroed, x0_turned, x0p_made = (sem("emb_turned"), sem("x0_made"), sem("x0_zeroed"),
                                                               sem("x0_turned"), sem("x0p_made"))
        blk_ones, blk_made, x2_turned, x2p_made = sem("blk_ones"), sem("blk_made"), sem("x2_turned"), sem("x2p_made")
        g_summed, g_made, z1_made, z2_summed, z2_made = (sem("g_summed"), sem("g_made"), sem("z1_made"),
                                                         sem("z2_summed"), sem("z2_made"))
        dense_turned, dense_made = sem("dense_turned"), sem("dense_made")
        h1_summed, h1_made, h2_summed, h2_made, y_summed, y_made = (
            sem("h1_summed"), sem("h1_made"), sem("h2_summed"), sem("h2_made"), sem("y_summed"), sem("y_made"))

        w1_view = raw.rearrange("h (j k) -> h j k", j=NF).rearrange("h j (l g) -> h j l g", g=NK1)
        turns = []

        def w1_source(J, K):
            return w1_view[:, J * JL:min(J * JL + JL, NF), :, K]

        for a, b_ in ((0, 4), (4, NT0 - 1), (NT0 - 1, NT0)):
            srcs = [w0_sym[:, DPT * t:min(DPT * t + DPT, ND), :].rearrange("p d j -> p (d j)") for t in range(a, b_)]
            turns.append((srcs, l0_rows(a), "w0", a))
        for kind, tiles in (("split", l1_split), ("whole", l1_whole)):
            a = 0
            while a < len(tiles):
                rows = JLAST * KL if tiles[a][0] == NJ - 1 else P
                b_ = a
                while b_ < len(tiles) and b_ - a < 4 and (tiles[b_][0] == NJ - 1) == (rows < P):
                    b_ += 1
                turns.append(([w1_source(*t) for t in tiles[a:b_]], rows, kind, a))
                a = b_
        last_w1_turn = len(turns)
        for a in range(0, NF, 4):
            js = list(range(a, min(a + 4, NF)))
            turns.append(([raw[:, j * H:(j + 1) * H] for j in js], P, "w2", a))
        turn_bank = [turn_x2_ps, g_ps[0], g_ps[1], z2_ps]
        first_bank = [turn_x2_ps, g_ps[0], g_ps[1], turn_x0]
        splits_upto = [sum(t[2] == "split" for t in turns[:g + 1]) for g in range(len(turns))]

        def turn_dst(kind, rows, a, n):
            dst = {"w0": w0_tiles, "split": w1_head, "whole": w1_whole, "w2": w2_tiles}[kind]
            return dst[0:rows, a:a + n, :]

        PE_TURN_X2, PE_G = 5, (9, 11, 13, 15)
        PE_EMB = (3, 8, 13, 18)
        PE_X0P = {3: (7, 12, 17), 4: (7,)}
        PE_DENSE = 10
        PE_Z2 = 18
        Z2_PER_UNIT = 4
        PE_Z2_END = PE_Z2 + -(-NF // Z2_PER_UNIT) - NU
        TAIL_LAG = 2
        DVE_LAG = 7
        LAG = 4

        def x0_parts(bank, part):
            dst = x0_sb[0:NF, :].rearrange("j (b d) -> j b d", d=D)[:, :, 4 * part:4 * part + 4]
            return dst.rearrange("j b m -> j m b"), bank[0:NF, :].rearrange("j (m b) -> j m b", m=4)

        def x0p_part(q, n):
            return PE_X0P[q].index(n) + (0 if q == 3 else len(PE_X0P[3]))

        def used(eng, st, i):
            split = is_split(i, st.q)
            wait(eng, split_used if split else whole_used, st.done(i, split))

        def k_rows(J):
            return JLAST * KL if J == NJ - 1 else P

        block = ctx.enter_context(nc.Block())

        @block.sync
        def _(sp):
            def settle():
                sp.sem_inc(sp_passed, 1)

            sp.dma_start(idx[:], ids[0:P, :]).then_inc(ld_idx_first, 16)
            sp.dma_start(ident[:], ident_in).then_inc(ld_const, 16)
            sp.dma_start(mask[:], mask_in).then_inc(ld_const, 16)
            for i, b_ in enumerate((b0, b1, b2)):
                sp.dma_start(bias[:, i:i + 1], b_.rearrange("(p o) -> p o", o=1)).then_inc(ld_const, 16)
            sp.dma_start(w0_raw, w0).then_inc(ld_w0, 16)
            sp.dma_start(raw, w1).then_inc(ld_w1, 16)

            def store_x0(c, cols, semaphore):
                dst = bass.ds(c * (P * D) + cols.start, cols.stop - cols.start)
                sp.dma_start(x0_dram[0:NF, dst], x0_sb[0:NF, cols]).then_inc(semaphore, 16)
                sp.dma_start(x0_dram[NF:ROWS_X0, dst], x0_sb[0:ROWS_X0 - NF, cols]).then_inc(semaphore, 16)

            def load_rep_j(st):
                settle()
                cols = bass.ds(st.count(N, 0), N)
                for J in range(NJ):
                    src = x0_dram[J * JL:(J + 1) * JL, cols].unsqueeze(1).to_broadcast([JL, KL, N])
                    sp.dma_start(rep_j[:, st.q % 2, J], src).then_inc(ld_rep_j[st.q % 2], 16)

            def load_rep_l0(st, tiles, semaphore):
                settle()
                for t in tiles:
                    first = DPT * max(t - 1, 0)
                    n = min(DPT, ND - first)
                    rows = x0_dram[first:first + NF, bass.ds(st.count(N, 0), N)]
                    src = bass.AP(tensor=rows.tensor, offset=rows.offset, dep_tracking_offset=rows.dep_tracking_offset,
                                  ap=[[B * D if t > 0 else 0, n], [B * D, NF], [1, N]])
                    sp.dma_start(rep_l0[0:n * NF, t], src).then_inc(semaphore, 16)

            def mults_done(st, i):
                settle()
                wait(sp, whole_ready, st.done(i, False))
                settle()
                wait(sp, full_ready, st.done(i, True))
                settle()

            def load_x1(st, half, semaphore):
                settle()
                src = x1_dram[bass.ds(st.count(1, 0), 1)].rearrange("s (l g) n -> (s l) g n", g=NK1)
                src = src[:, half * 4:half * 4 + 4, :].rearrange("l g n -> l (g n)").unsqueeze(0).to_broadcast([JL, KL, 4 * N])
                sp.dma_start(rep_x1[:, half * 4:half * 4 + 4, :], src).then_inc(semaphore, 16)

            def store_x1(st):
                wait(sp, x1_made, st.count(1, 1))
                settle()
                dst = x1_dram[bass.ds(st.count(1, 0), 1)].rearrange("s k n -> (s k) n")
                sp.dma_start(dst, x1_sb[:]).then_inc(x1_stored, 16)
                wait(sp, x1_stored, st.count(16, 16))
                settle()

            for t in range(2):
                sp.dma_start(wt3[:, t:t + 1], w_top3[t * P:(t + 1) * P]).then_inc(ld_dense, 16)
            for t in range(6):
                b_ = b_top1[t * P:(t + 1) * P] if t < 4 else b_top2[(t - 4) * P:(t - 3) * P]
                sp.dma_start(bias_top[:, t:t + 1], b_.rearrange("(p o) -> p o", o=1)).then_inc(ld_dense, 16)
            sp.wait_ge(w_turned, last_w1_turn)
            sp.dma_start(raw, w2).then_inc(ld_w2, 16)

            sp.wait_ge(x0_made, 4)
            store_x0(0, slice(0, N), first_stored)
            sp.wait_ge(first_stored, 32)
            load_rep_l0(Step(0, 0), range(3), ld_first)
            load_rep_l0(Step(0, 0), range(3, 5), ld_second)
            load_rep_l0(Step(0, 0), range(5, 1 + NT0), ld_rep_l0)
            store_x0(0, slice(N, P * D), x0_stored)
            load_rep_j(Step(0, 0))
            sp.wait_ge(x0_stored, 32)
            mults_done(Step(0, -1), None)
            load_rep_l0(Step(0, 1), range(1 + NT0), ld_rep_l0)
            store_x1(Step(0, 0))
            load_x1(Step(0, 0), 0, ld_x1_a)
            load_x1(Step(0, 0), 1, ld_x1_b)
            load_rep_j(Step(0, 1))
            store_x1(Step(0, 1))
            mults_done(Step(0, 0), A_LAST)
            load_x1(Step(0, 1), 0, ld_x1_a)

            def step(c, q, has_next=True, chunk_after=False):
                st, prev, nxt = Step(c, q, has_next), Step(c, q - 1), Step(c, q + 1)
                mults_done(prev, None)
                if not has_next:
                    load_x1(st, 1, ld_x1_b)
                    sp.dma_start(wt1[:, 0:3, :], w_top1[0:3 * P].rearrange("(t p) m -> p t m", p=P)).then_inc(ld_top, 16)
                    sp.dma_start(wt1[0:16, 3, :], w_top1[3 * P:3 * P + 16]).then_inc(ld_top, 16)
                    sp.dma_start(wt2, w_top2.rearrange("(t p) m -> p t m", p=P)).then_inc(ld_top, 16)
                    sp.dma_start(dense, dense_ctx.rearrange("(c p) f -> p c f", p=P)).then_inc(ld_top, 16)
                    return
                if q == 3 and chunk_after:
                    wait(sp, x0_stored, c * 32 + 64)
                load_rep_l0(nxt, range(1 + NT0), ld_rep_l0)
                load_x1(st, 1, ld_x1_b)
                load_rep_j(nxt)
                store_x1(nxt)
                mults_done(st, A_LAST)
                load_x1(nxt, 0, ld_x1_a)
                if q == 2 and chunk_after:
                    wait(sp, x0_made, c * 4 + 8)
                    settle()
                    store_x0(c + 1, slice(0, P * D), x0_stored)

            step(0, 1)
            with sp.Fori(0, CH - 1) as c:
                for q in range(2, 6):
                    step(c, q, chunk_after=True)
            for q in range(2, 4):
                step(CH - 1, q, has_next=q < 3)
            sp.wait_ge(y_made, 1)
            sp.dma_start(out.rearrange("b o -> o b"), y_sb).then_inc(out_stored, 16)
            sp.wait_ge(out_stored, 16)

        @block.gpsimd
        def _(pool):
            def gather(c):
                if isinstance(c, int) and c == 0:
                    pool.wait_ge(ld_idx_first, 16)
                else:
                    pool.wait_ge(gathered, c * (16 * NF))
                    pool.dma_start(idx[:], ids[bass.ds(c * P, P), :]).then_inc(ld_idx, 16)
                    pool.wait_ge(ld_idx, c * 16)
                    pool.wait_ge(emb_turned, c * 4)
                pool.sem_inc(pool_passed, 1)
                for f in range(NF):
                    pool.indirect_dma_start(
                        out=emb[:, f, :], out_offset=None, in_=tables[f],
                        in_offset=bass.IndirectOffsetOnAxis(ap=idx[:, f:f + 1].bitcast(U32), axis=0)
                    ).then_inc(gathered, 16)

            gather(0)
            with pool.Fori(1, CH) as c:
                gather(c)

        @block.tensor
        def _(pe):
            turned = [0]

            def turn_weights(g):
                srcs, rows, kind, _ = turns[g]
                if g >= len(turn_bank):
                    old = g - len(turn_bank)
                    pe.wait_ge(w_copied, old + 1)
                    wait(pe, w_tailed, splits_upto[old])
                for m, src in enumerate(srcs):
                    mm = pe.transpose(turn_bank[g % len(turn_bank)][0:rows, m * P:(m + 1) * P], src, ident[:])
                mm.then_inc(w_turned, 1)

            def turn_first(part):
                for m in range(4):
                    mm = pe.transpose(first_bank[part][0:NF, m * P:(m + 1) * P], emb[:, :, 4 * part + m], ident[:])
                mm.then_inc(emb_turned, 1)

            def turn_emb(c, part):
                if part == 0:
                    pe.wait_ge(gathered, c * (16 * NF) + 16 * NF)
                    wait(pe, x0p_made, c * 4)
                wait(pe, x0_made, c * 4 + part)
                pe.sem_inc(pe_passed, 1)
                for m in range(4):
                    mm = pe.transpose(turn_x0[0:NF, m * P:(m + 1) * P], emb[:, :, 4 * part + m], ident[:])
                mm.then_inc(emb_turned, 1)

            def turn_x0p(c, part):
                if part == 0:
                    pe.wait_ge(x0_made, c * 4 + 4)
                wait(pe, x0p_made, c * 4 + part)
                for m in range(GRP):
                    g = part * GRP + m
                    mm = pe.transpose(turn_x0[:, m * P:(m + 1) * P], x0_sb[:, g * P:(g + 1) * P], ident[:])
                mm.then_inc(x0_turned, 1)

            def unit(st, i):
                kind, u = UNITS[i]
                split = is_split(i, st.q)
                count, at = st.place(i, split)
                slot = at % (RING_S if split else RING_W)
                wait(pe, tail_ready if split else whole_ready, count + 1)
                if kind == "L0":
                    tiles = [(w0_tiles[0:l0_rows(t), t], l0_rows(t), t == 0, t == NT0 - 1)
                             for t in range(u[0], u[0] + u[1])]
                    acc = acc0
                    if i == L0_FIRST:
                        wait(pe, x1_made, st.count(1, 1))
                else:
                    J, K = u
                    tiles = []
                    for m in range(2):
                        r, first = k_rows(J), i == 0 and m == 0
                        last = i == NU - 1 and m == 1
                        if split:
                            n = l1_split.index((J, K + m))
                            tiles.append(((w1_head[0:r, n], w1_tail[0:r, n]), r, first, last))
                        else:
                            tiles.append((w1_whole[0:r, l1_whole.index((J, K + m))], r, first, last))
                    acc = acc1[st.q % 2]
                    if i == 0:
                        wait(pe, x2_made, st.count(1, -1))
                for m, (w, r, first, last) in enumerate(tiles):
                    if split:
                        head, tail = z_head[0:r, slot, m], z_tail[0:r, slot, m]
                        pe.matmul(acc[:], w[0], head, start=first, stop=False)
                        pe.matmul(acc[:], w[0], tail, start=False, stop=False)
                        mm = pe.matmul(acc[:], w[1], head, start=False, stop=last)
                    else:
                        mm = pe.matmul(acc[:], w, z_whole[0:r, slot, m], start=first, stop=last)
                mm.then_inc(split_used if split else whole_used, 1)

            def turn_x2(st):
                wait(pe, x2_made, st.count(1, 1))
                wait(pe, x2p_made, st.count(1, 0))
                for g in range(GRP):
                    mm = pe.transpose(turn_x2_ps[:, g * P:(g + 1) * P], x2_sb[:, g * P:(g + 1) * P], ident[:])
                mm.then_inc(x2_turned, 1)

            def g_products(st, groups):
                if groups[0] == 0:
                    wait(pe, x2p_made, st.count(1, 1))
                    wait(pe, blk_made, st.count(1, 1))
                for g in groups:
                    if g >= 2:
                        pe.wait_ge(g_made, st.count(GRP, g - 1))
                    pe.matmul(g_ps[g % 2][:, 0:NG * GB], x2_p[:, g], x0_blk[:, g].rearrange("p j b -> p (j b)"),
                              start=True, stop=True).then_inc(g_summed, 1)

            def l2_products(c, js):
                if js[0] == 0:
                    wait(pe, g_made, c * (GRP * SPC) + GRP * SPC)
                for j in js:
                    mm = pe.matmul(z2_ps[:, bass.ds(c * P, P)], w2_tiles[:, j], g_sum[:, j, :], start=j == 0, stop=j == NF - 1)
                if js[-1] == NF - 1:
                    mm.then_inc(z2_summed, 1)

            def step(c, q, has_next=True, chunk_next=None):
                st, prev = Step(c, q, has_next), Step(c, q - 1)
                for n, i in enumerate(st.units()):
                    if not has_next and n == PE_DENSE:
                        pe.wait_ge(ld_top, 16 * 4)
                        for m in range(CH):
                            mm = pe.transpose(turn_x0[0:16, m * P:(m + 1) * P], dense[:, m], ident[:])
                        mm.then_inc(dense_turned, 1)
                    if not (st.static and c * SPC + q == 0):
                        if n == PE_TURN_X2:
                            turn_x2(prev)
                        if n in PE_G:
                            g_products(prev, (PE_G.index(n),))
                    if q == 2 and chunk_next is not None and n in PE_EMB:
                        turn_emb(chunk_next, PE_EMB.index(n))
                    if chunk_next is not None and n in PE_X0P.get(q, ()):
                        turn_x0p(chunk_next, x0p_part(q, n))
                    if q in (4, 5):
                        first = (n - PE_Z2 + (q - 4) * NU) * Z2_PER_UNIT
                        if 0 <= first < NF:
                            l2_products(c, range(first, min(first + Z2_PER_UNIT, NF)))
                    unit(st, i)

            pe.wait_ge(ld_const, 16 * 5)
            pe.wait_ge(w0_staged, 2 * ND - 1)
            for g in range(last_w1_turn):
                if turns[g][2] != "w0":
                    pe.wait_ge(ld_w1, 16)
                turn_weights(g)
            pe.wait_ge(ld_w2, 16)
            for g in range(last_w1_turn, len(turns)):
                turn_weights(g)
            pe.wait_ge(ld_dense, 16 * 8)
            pe.wait_ge(w_copied, len(turns))
            wait(pe, w_tailed, splits_upto[-1])
            pe.wait_ge(gathered, 16 * NF)
            for part in range(4):
                turn_first(part)
            first = Step(0, -1)
            for i in first.units():
                unit(first, i)
            for part in range(SPC):
                turn_x0p(0, part)
            step(0, 0)
            step(0, 1)
            with pe.Fori(0, CH - 1) as c:
                for q in range(2, 6):
                    step(c, q, chunk_next=c + 1)
            for q in range(2, 4):
                step(CH - 1, q, has_next=q < 3)

            last = Step(CH - 1, 3, False)

            def top1(m, t, **flags):
                rhs = (z0[:], z1[:], z2, dense_t)[t]
                w = wt1[0:16, 3, m * P:(m + 1) * P] if t == 3 else wt1[:, t, m * P:(m + 1) * P]
                return pe.matmul(h1_ps[m][:], w, rhs, **{"start": False, "stop": False, **flags})

            pe.wait_ge(z0_made, STEPS)
            pe.wait_ge(dense_made, 1)
            top1(0, 3, start=True)
            top1(0, 0)
            turn_x2(last)
            top1(1, 3, start=True)
            top1(1, 0)
            g_products(last, (0, 1))
            top1(2, 3, start=True)
            top1(2, 0)
            g_products(last, (2, 3))
            top1(3, 3, start=True)
            top1(3, 0)
            pe.wait_ge(z1_made, CH)
            for m in range(4):
                top1(m, 1)
            l2_products(CH - 1, range(NF))
            pe.wait_ge(z2_made, 1)
            for m in range(4):
                top1(m, 2, stop=True).then_inc(h1_summed, 1)
            for t in range(4):
                pe.wait_ge(h1_made, t + 1)
                for m in range(2):
                    mm = pe.matmul(g_ps[m][:], wt2[:, t, m * P:(m + 1) * P], h1[:, t], start=t == 0, stop=t == 3)
                    if t == 3:
                        mm.then_inc(h2_summed, 1)
            for t in range(2):
                pe.wait_ge(h2_made, t + 1)
                mm = pe.matmul(turn_x2_ps[0:1, :], wt3[:, t:t + 1], h2[:, t], start=t == 0, stop=t == 1)
            mm.then_inc(y_summed, 1)

        @block.vector
        def _(dve):
            nc.vector.memset(x0_sb[:], 0.0).then_inc(x0_zeroed, 1)
            dve.wait_ge(ld_w0, 16)

            def diagonal(start, n):
                return w0_raw[:, start:start + (NF + 1) * (n - 1) + 1:NF + 1]

            nc.vector.tensor_copy(w0_sym[:, 0, :], diagonal(0, NF)).then_inc(w0_staged, 1)
            for d in range(1, ND):
                nc.vector.tensor_tensor(w0_sym[:, d, 0:NF - d], diagonal(d, NF - d), diagonal(NF * d, NF - d),
                                        ALU.add).then_inc(w0_staged, 1)
                nc.vector.tensor_tensor(w0_sym[:, d, NF - d:NF], diagonal(NF * (NF - d), d), diagonal(NF - d, d),
                                        ALU.add).then_inc(w0_staged, 1)
            dve.wait_ge(ld_const, 16 * 5)
            nc.vector.tensor_scalar(bias16[:], bias[:, 2:3], float(D), None, ALU.mult).then_inc(b2_scaled, 1)
            for g in range(GRP):
                nc.vector.tensor_copy(x0_blk[:, g, NF, :], mask[:]).then_inc(blk_ones, 1)
            n = 0
            for g, (srcs, rows, kind, a) in enumerate(turns):
                if kind == "split":
                    dve.wait_ge(w_copied, g + 1)
                    m = len(srcs)
                    nc.vector.tensor_tensor(
                        w1_tail[0:rows, a:a + m], turn_bank[g % len(turn_bank)][0:rows, 0:m * P].rearrange(
                            "p (t h) -> p t h", t=m),
                        w1_head[0:rows, a:a + m].bitcast(F32), ALU.subtract).then_inc(w_tailed, 1)

            def operands(st, i):
                kind, u = UNITS[i]
                if kind == "L0":
                    t, n = u
                    r = l0_rows(t)
                    return rep_l0[0:r, 0:1].to_broadcast([r, n, N]), rep_l0[0:r, 1 + t:1 + t + n]
                J, K = u
                return rep_j[:, st.q % 2, J:J + 1].to_broadcast([P, 2, N]), rep_x1[:, K:K + 2]

            def tail(st, i):
                count, at = st.place(i, True)
                slot = at % RING_S
                dve.wait_ge(head_ready, count + 1)
                wait(dve, split_used, count + (1 - RING_S))
                nc.vector.tensor_tensor(z_tail[:, slot], z_full[:, at % RING_F],
                                        z_head[:, slot].bitcast(F32), ALU.subtract).then_inc(tail_ready, 1)

            def product(st, i):
                split = is_split(i, st.q)
                count, at = st.place(i, split)
                slot = at % (RING_F if split else RING_W)
                if st.q == -1 and i == L0_FIRST:
                    dve.wait_ge(ld_first, 16 * 3)
                elif st.q == -1 and UNITS[i][1] == L0_UNITS[1]:
                    dve.wait_ge(ld_second, 16 * 2)
                elif st.q == -1 and UNITS[i][1] == L0_UNITS[2]:
                    dve.wait_ge(ld_rep_l0, 16 * (NT0 - 4))
                elif i == L0_FIRST:
                    dve.wait_ge(ld_rep_l0, st.count(16 * (1 + NT0), 32 * (1 + NT0) - 16 * 5))
                if i == 0:
                    dve.wait_ge(ld_rep_j[st.q % 2], st.c * (16 * NJ * SPC // 2) + 16 * NJ * (st.q // 2 + 1))
                    dve.wait_ge(ld_x1_a, st.count(16, 16))
                if i == B_FIRST:
                    dve.wait_ge(ld_x1_b, st.count(16, 16))
                in0, in1 = operands(st, i)
                rows, tiles = in0.shape[0], in0.shape[1]
                if split:
                    wait(dve, tail_ready, count + (1 - RING_F))
                    nc.vector.tensor_tensor(z_full[:, slot], in0, in1, ALU.mult).then_inc(full_ready, 1)
                else:
                    wait(dve, whole_used, count + (1 - RING_W))
                    nc.vector.tensor_tensor(z_whole[0:rows, slot, 0:tiles], in0, in1, ALU.mult).then_inc(whole_ready, 1)

            def sum_x1(st):
                dve.wait_ge(x1_made, st.count(1, 1))
                nc.vector.tensor_reduce(z0[:, bass.ds(st.count(BS, 0), BS)], x1_sb[:].rearrange("p (b d) -> p b d", d=D),
                                        AX.X, ALU.add).then_inc(z0_made, 1)

            def step(c, q, has_next=True):
                st = Step(c, q, has_next)
                late = []
                order = st.units()
                for n, i in enumerate(order):
                    if is_split(i, q) and len(late) == RING_F:
                        tail(st, late.pop(0))
                    product(st, i)
                    if late and (order.index(late[0]) <= n - TAIL_LAG):
                        tail(st, late.pop(0))
                    if is_split(i, q):
                        late.append(i)
                    if st.static and c * SPC + q == 0 and n == order.index(L0_LAST):
                        sum_x1(st)
                    if has_next and q >= 0 and n == order.index(L0_LAST) + DVE_LAG:
                        sum_x1(Step(c, q + 1))
                for i in late:
                    tail(st, i)

            for part in (1, 3):
                dve.wait_ge(emb_turned, part + 1)
                dst, src = x0_parts(first_bank[part], part)
                nc.vector.tensor_copy(dst, src).then_inc(x0_made, 1)
            dve.wait_ge(w_turned, sum(t[2] == "w0" for t in turns))
            step(0, -1)
            step(0, 0)
            step(0, 1)
            with dve.Fori(0, CH - 1) as c:
                for q in range(2, 6):
                    step(c, q)
            for q in range(2, 4):
                step(CH - 1, q, has_next=q < 3)

        @block.scalar
        def _(act):
            act.wait_ge(ld_const, 16 * 5)

            def copy_turned(g):
                srcs, rows, kind, a = turns[g]
                act.wait_ge(w_turned, g + 1)
                m = len(srcs)
                nc.scalar.activation(turn_dst(kind, rows, a, m),
                                     turn_bank[g % len(turn_bank)][0:rows, 0:m * P].rearrange("p (t h) -> p t h", t=m),
                                     ACT.Copy).then_inc(w_copied, 1)

            def copy_emb(c, part):
                if part == 0:
                    wait(act, x0_stored, c * 32)
                    wait(act, x0_turned, c * SPC)
                act.wait_ge(emb_turned, c * 4 + (part + 1))
                dst, src = x0_parts(turn_x0, part)
                nc.scalar.activation(dst, src, ACT.Copy).then_inc(x0_made, 1)

            def copy_x0p(c, part):
                act.wait_ge(x0_turned, c * SPC + (part + 1))
                nc.scalar.activation(x0_p[:, part * GRP:(part + 1) * GRP, :],
                                     turn_x0[:].rearrange("p (g j) -> p g j", g=GRP)[:, :, 0:NF],
                                     ACT.Copy).then_inc(x0p_made, 1)

            def make_x1(st):
                used(act, Step(st.c, st.q - 1), L0_LAST)
                wait(act, x1_stored, st.count(16, 0))
                wait(act, z0_made, st.count(1, 0))
                nc.scalar.activation(x1_sb[:], acc0[:], ACT.Identity, bias=bias[:, 0:1]).then_inc(x1_made, 1)

            def make_x2(st):
                used(act, st, NU - 1)
                wait(act, x2_turned, st.count(1, 0))
                nc.scalar.activation(x2_sb[:], acc1[st.q % 2][:], ACT.Identity, bias=bias[:, 1:2]).then_inc(x2_made, 1)

            def make_blk(st):
                wait(act, g_summed, st.count(GRP, 0))
                part = st.q % SPC
                act.wait_ge(x0p_made, st.count(1, SPC - part))
                for b_ in range(GB):
                    ins = nc.scalar.activation(x0_blk[:, :, 0:NF, b_], x0_p[:, part * GRP:(part + 1) * GRP, :], ACT.Copy,
                                               scale=mask[:, b_:b_ + 1])
                ins.then_inc(blk_made, 1)

            def make_x2p(st):
                act.wait_ge(x2_turned, st.count(1, 1))
                wait(act, g_summed, st.count(GRP, 0))
                nc.scalar.activation(x2_p[:], turn_x2_ps[:].rearrange("p (g h) -> p g h", g=GRP),
                                     ACT.Copy).then_inc(x2p_made, 1)

            def copy_g(st, groups):
                if st.q % SPC == 0 and groups[0] == 0:
                    assert PE_Z2_END <= PE_G[0]
                    wait(act, z2_summed, st.c + st.q // SPC)
                for g in groups:
                    act.wait_ge(g_summed, st.count(GRP, g + 1))
                    b_ = (st.q % SPC) * BS + g * GB
                    nc.scalar.activation(g_sum[:, :, b_:b_ + GB],
                                         g_ps[g % 2][:, 0:NG * GB].rearrange("p (j b) -> p j b", b=GB),
                                         ACT.Copy).then_inc(g_made, 1)

            def make_z1(c):
                act.wait_ge(g_made, c * (SPC * GRP) + SPC * GRP)
                nc.scalar.activation(z1[:, bass.ds(c * P, P)], g_sum[:, NF, :], ACT.Copy).then_inc(z1_made, 1)

            def head(st, i):
                count, at = st.place(i, True)
                slot = at % RING_S
                act.wait_ge(full_ready, count + 1)
                wait(act, split_used, count + (1 - RING_S))
                nc.scalar.activation(z_head[:, slot], z_full[:, at % RING_F], ACT.Copy).then_inc(head_ready, 1)

            def step(c, q, has_next=True, chunk_next=None):
                st, prev = Step(c, q, has_next), Step(c, q - 1)
                first = st.static and c * SPC + q == 0
                order = st.units()
                for n, i in enumerate(order):
                    if is_split(i, q):
                        head(st, i)
                    if not first:
                        if n == 2:
                            make_x2(prev)
                        if n == 3:
                            make_blk(prev)
                        if n == PE_TURN_X2 + LAG:
                            make_x2p(prev)
                        if n - LAG in PE_G:
                            copy_g(prev, (PE_G.index(n - LAG),))
                    if q == 2 and chunk_next is not None and n - LAG in PE_EMB:
                        copy_emb(chunk_next, PE_EMB.index(n - LAG))
                    if chunk_next is not None and n - LAG in PE_X0P.get(q, ()):
                        copy_x0p(chunk_next, x0p_part(q, n - LAG))
                    if not has_next and n == PE_DENSE + LAG:
                        act.wait_ge(dense_turned, 1)
                        nc.scalar.activation(dense_t, turn_x0[0:16, :], ACT.Copy).then_inc(dense_made, 1)
                    if has_next and n == order.index(L0_LAST) + LAG:
                        make_x1(Step(c, q + 1))
                    if q == 4 and n == PE_G[-1] + LAG + 1:
                        make_z1(c)

            for g in range(len(turns)):
                copy_turned(g)
            act.wait_ge(x0_zeroed, 1)
            for part in (0, 2):
                act.wait_ge(emb_turned, part + 1)
                dst, src = x0_parts(first_bank[part], part)
                nc.scalar.activation(dst, src, ACT.Copy).then_inc(x0_made, 1)
            make_x1(Step(0, 0))
            for part in range(SPC):
                copy_x0p(0, part)
            act.wait_ge(blk_ones, GRP)
            act.wait_ge(b2_scaled, 1)
            step(0, 0)
            step(0, 1)
            with act.Fori(0, CH - 1) as c:
                for q in range(2, 6):
                    step(c, q, chunk_next=c + 1)
            for q in range(2, 4):
                step(CH - 1, q, has_next=q < 3)
            last = Step(CH - 1, 3, False)
            make_x2(last)
            make_blk(last)
            make_x2p(last)
            copy_g(last, (0, 1))
            copy_g(last, (2, 3))
            make_z1(CH - 1)
            act.wait_ge(z2_summed, CH)
            nc.scalar.activation(z2, z2_ps[:], ACT.Identity, bias=bias16[:]).then_inc(z2_made, 1)
            for t in range(4):
                act.wait_ge(h1_summed, t + 1)
                nc.scalar.activation(h1[:, t], h1_ps[t][:], ACT.Relu, bias=bias_top[:, t:t + 1]).then_inc(h1_made, 1)
            for t in range(2):
                act.wait_ge(h2_summed, t + 1)
                nc.scalar.activation(h2[:, t], g_ps[t][:], ACT.Relu, bias=bias_top[:, 4 + t:5 + t]).then_inc(h2_made, 1)
            act.wait_ge(y_summed, 1)
            nc.scalar.activation(y_sb, turn_x2_ps[0:1, :], ACT.Copy).then_inc(y_made, 1)


def kernel(**inputs):
    import numpy as _np
    import concourse.bacc as _bacc
    from concourse import mybir as _mybir
    from concourse.bass_utils import run_bass_kernel_spmd as _run

    nc = _bacc.Bacc("TRN2", target_bir_lowering=False, num_devices=1)
    arrays = {}

    def take(name, a):
        a = _np.ascontiguousarray(a)
        arrays[f"in_{name}"] = a
        return nc.dram_tensor(f"in_{name}", a.shape, _mybir.dt.from_np(a.dtype), kind="ExternalInput").ap()

    ap = {name: take(name, a) for name, a in inputs.items()}
    ident = take("ident", _np.eye(128, dtype=_np.float32))
    mask = take("mask", _np.repeat(_np.eye(8, dtype=_np.float32), 16, axis=0))
    out = nc.dram_tensor("out", (512, 1), _mybir.dt.float32, kind="ExternalOutput").ap()
    build(nc, ap["dense_ctx"], ap["ids"], [ap[f"tbl_{f}"] for f in range(39)], ap["W_top1"], ap["b_top1"],
          ap["W_top2"], ap["b_top2"], ap["W_top3"], ap["L0_rec_W0"], ap["L0_rec_b0"], ap["L0_rec_W1"],
          ap["L0_rec_b1"], ap["L0_rec_W2"], ap["L0_rec_b2"], ident, mask, out)
    r = _run(nc, [arrays], core_ids=[0])
    return r.results[0]["out"]
```
